# Optimizing a Trainium2 kernel written in Bass

```python
import numpy as np
import jax
import jax.numpy as jnp

def _softmax(x, axis=-1):
    return jax.nn.softmax(x, axis=axis)

def _gelu(x):
    return jax.nn.gelu(x, approximate=True)

def _silu(x):
    return jax.nn.silu(x)

def _sigmoid(x):
    return jax.nn.sigmoid(x)

def _layernorm(x, axis=-1, eps=1e-05):
    m = jnp.mean(x, axis=axis, keepdims=True)
    v = jnp.var(x, axis=axis, keepdims=True)
    return (x - m) / jnp.sqrt(v + eps)

def _scatter_add(tgt, idx, src, axis=0):
    return tgt.at[idx].add(src)

def _segment_sum(src, seg, n):
    return jax.ops.segment_sum(src, seg, n)
kernel_name = 'mk_xattn_ffn_d1_seqx_r4_45b9cc'

def setup_inputs(seed: int=0):
    np.random.seed(seed)
    _w = jnp.asarray

    def _rec_inputs():
        import jax
        import jax.numpy as jnp
        _rk = jax.random.key(seed)
        x = 7.22e-05 + 1 * jax.random.normal(jax.random.fold_in(_rk, 1), (2, 1024, 256), jnp.float32)
        _lenS = 1024 - jax.random.randint(jax.random.fold_in(_rk, 7), (2,), 0, max(1, 1024 // 4) + 1, jnp.int32)
        _lenS2 = 77 - jax.random.randint(jax.random.fold_in(_rk, 8), (2,), 0, max(1, 77 // 4) + 1, jnp.int32)
        _ctx_768P = jax.random.normal(jax.random.fold_in(_rk, 11), (2, 16, 192), jnp.float32)
        _ctx_768c = jax.random.dirichlet(jax.random.fold_in(_rk, 511), 0.3 * jnp.ones((16,), jnp.float32), (2, 77))
        _ctx_768t = jnp.einsum('bsk,bkd->bsd', _ctx_768c, _ctx_768P)
        _ctx_768t = _ctx_768t * jax.lax.rsqrt(jnp.mean(jnp.square(_ctx_768t)) + 1e-12) * 0.953939
        ctx_768 = -0.000191848 + 0.999787 * (_ctx_768t + 0.3 * jax.random.normal(jax.random.fold_in(_rk, 611), (2, 77, 192), jnp.float32))
        return (x, ctx_768)
    x, ctx_768 = _rec_inputs()

    def _L0_xattn_setup():
        import jax, jax.numpy as jnp
        import numpy as np
        HEADS = 8
        DIM_HEAD = 64
        SCALE = DIM_HEAD ** (-0.5)
        key = jax.random.key(seed)
        ks = jax.random.split(key, 7)
        B, Nq, Nc = (4, 512, 512)
        Dq, Dc = (256, 192)
        inner = HEADS * DIM_HEAD
        x = jax.random.normal(ks[0], (B, Nq, Dq), dtype=jnp.float32)
        context = jax.random.normal(ks[1], (B, Nc, Dc), dtype=jnp.float32)
        Wq = jax.random.normal(ks[2], (Dq, inner), dtype=jnp.float32) * Dq ** (-0.5)
        Wk = jax.random.normal(ks[3], (Dc, inner), dtype=jnp.float32) * Dc ** (-0.5)
        Wv = jax.random.normal(ks[4], (Dc, inner), dtype=jnp.float32) * Dc ** (-0.5)
        Wo = jax.random.normal(ks[5], (inner, Dq), dtype=jnp.float32) * inner ** (-0.5)
        bo = jax.random.normal(ks[6], (Dq,), dtype=jnp.float32) * 0.01
        return {'x': x, 'context': context, 'Wq': Wq, 'Wk': Wk, 'Wv': Wv, 'Wo': Wo, 'bo': bo}
    _L0_xattn_all = _L0_xattn_setup()
    _L0_xattn_in = {k: v for k, v in _L0_xattn_all.items() if k in ('Wq', 'Wk', 'Wv', 'Wo', 'bo')}
    del _L0_xattn_all

    def _L0_ffn_setup():
        import jax, jax.numpy as jnp
        import numpy as np
        B, S, H, F, G = (8, 512, 256, 1024, 128)
        EPS = 1e-05

        def _dequant(q, scales, g):
            K, N = q.shape
            w = (q.astype(jnp.float32) - 128.0).reshape(K // g, g, N) * scales[:, None, :]
            return w.reshape(K, N)
        key = jax.random.key(seed)
        ks = jax.random.split(key, 8)
        x = jax.random.normal(ks[0], (B, S, H), dtype=jnp.float32)
        ln_gamma = jnp.ones((H,), jnp.float32)
        ln_beta = jnp.zeros((H,), jnp.float32)
        fc1_q = jax.random.randint(ks[1], (H, F), 0, 64, dtype=jnp.int32)
        fc2_q = jax.random.randint(ks[2], (F, H), 0, 64, dtype=jnp.int32)
        fc1_scales = jax.random.uniform(ks[3], (H // G, F), jnp.float32) * 0.02 + 0.001
        fc2_scales = jax.random.uniform(ks[4], (F // G, H), jnp.float32) * 0.02 + 0.001
        fc1_bias = jax.random.normal(ks[5], (F,), jnp.float32) * 0.02
        fc2_bias = jax.random.normal(ks[6], (H,), jnp.float32) * 0.02
        return {'x': x, 'ln_gamma': ln_gamma, 'ln_beta': ln_beta, 'fc1_q': fc1_q, 'fc1_scales': fc1_scales, 'fc1_bias': fc1_bias, 'fc2_q': fc2_q, 'fc2_scales': fc2_scales, 'fc2_bias': fc2_bias}
    _L0_ffn_all = _L0_ffn_setup()
    _L0_ffn_in = {k: v for k, v in _L0_ffn_all.items() if k in ('ln_gamma', 'ln_beta', 'fc1_q', 'fc1_scales', 'fc1_bias', 'fc2_q', 'fc2_scales', 'fc2_bias')}
    del _L0_ffn_all
    return {'x': x, 'ctx_768': ctx_768, 'L0_xattn_Wq': _L0_xattn_in['Wq'], 'L0_xattn_Wk': _L0_xattn_in['Wk'], 'L0_xattn_Wv': _L0_xattn_in['Wv'], 'L0_xattn_Wo': _L0_xattn_in['Wo'], 'L0_xattn_bo': _L0_xattn_in['bo'], 'L0_ffn_ln_gamma': _L0_ffn_in['ln_gamma'], 'L0_ffn_ln_beta': _L0_ffn_in['ln_beta'], 'L0_ffn_fc1_q': _L0_ffn_in['fc1_q'], 'L0_ffn_fc1_scales': _L0_ffn_in['fc1_scales'], 'L0_ffn_fc1_bias': _L0_ffn_in['fc1_bias'], 'L0_ffn_fc2_q': _L0_ffn_in['fc2_q'], 'L0_ffn_fc2_scales': _L0_ffn_in['fc2_scales'], 'L0_ffn_fc2_bias': _L0_ffn_in['fc2_bias']}

def reference(x, ctx_768, L0_xattn_Wq, L0_xattn_Wk, L0_xattn_Wv, L0_xattn_Wo, L0_xattn_bo, L0_ffn_ln_gamma, L0_ffn_ln_beta, L0_ffn_fc1_q, L0_ffn_fc1_scales, L0_ffn_fc1_bias, L0_ffn_fc2_q, L0_ffn_fc2_scales, L0_ffn_fc2_bias):
    import jax
    import jax.numpy as jnp

    def _L0_xattn_ref(x, context, Wq, Wk, Wv, Wo, bo):
        import jax, jax.numpy as jnp
        import numpy as np
        HEADS = 8
        DIM_HEAD = 64
        SCALE = DIM_HEAD ** (-0.5)
        B, Nq, _ = x.shape
        q = (x @ Wq).reshape(B, Nq, HEADS, DIM_HEAD)
        k = (context @ Wk).reshape(B, context.shape[1], HEADS, DIM_HEAD)
        v = (context @ Wv).reshape(B, context.shape[1], HEADS, DIM_HEAD)
        sim = jnp.einsum('bihd,bjhd->bhij', q, k) * SCALE
        attn = jax.nn.softmax(sim, axis=-1)
        out = jnp.einsum('bhij,bjhd->bihd', attn, v)
        out = out.reshape(B, Nq, HEADS * DIM_HEAD)
        return out @ Wo + bo

    def _L0_ffn_ref(x, ln_gamma, ln_beta, fc1_q, fc1_scales, fc1_bias, fc2_q, fc2_scales, fc2_bias):
        import jax, jax.numpy as jnp
        import numpy as np
        B, S, H, F, G = (8, 512, 256, 1024, 128)
        EPS = 1e-05

        def _dequant(q, scales, g):
            K, N = q.shape
            w = (q.astype(jnp.float32) - 128.0).reshape(K // g, g, N) * scales[:, None, :]
            return w.reshape(K, N)
        residual = x
        mu = jnp.mean(x, axis=-1, keepdims=True)
        var = jnp.mean(jnp.square(x - mu), axis=-1, keepdims=True)
        h = (x - mu) * jax.lax.rsqrt(var + EPS) * ln_gamma + ln_beta
        hf = h.reshape(-1, H)
        w1 = _dequant(fc1_q, fc1_scales, G)
        y = hf @ w1 + fc1_bias
        y = jax.nn.silu(y)
        w2 = _dequant(fc2_q, fc2_scales, G)
        z = y @ w2 + fc2_bias
        return residual + 0.5 * z.reshape(residual.shape)
    x = x + _L0_xattn_ref(_layernorm(x, axis=-1), ctx_768, L0_xattn_Wq, L0_xattn_Wk, L0_xattn_Wv, L0_xattn_Wo, L0_xattn_bo)
    x = x + _L0_ffn_ref(_layernorm(x, axis=-1), L0_ffn_ln_gamma, L0_ffn_ln_beta, L0_ffn_fc1_q, L0_ffn_fc1_scales, L0_ffn_fc1_bias, L0_ffn_fc2_q, L0_ffn_fc2_scales, L0_ffn_fc2_bias)
    return x

_drawn_inputs = setup_inputs


def setup_inputs(seed=0):
    import zlib

    import numpy as np

    out = dict(_drawn_inputs(seed))
    spreads = {'L0_ffn_ln_gamma': (1.0, 0.2), 'L0_ffn_ln_beta': (0.0, 0.1)}
    factors = {'L0_xattn_bo': 8.0, 'L0_ffn_fc1_bias': 8.0, 'L0_ffn_fc2_bias': 8.0}
    for name, (base, spread) in spreads.items():
        noise = np.random.default_rng([zlib.crc32(name.encode()), seed]).standard_normal(out[name].shape)
        drawn = base * np.exp(spread * noise) if base else spread * noise
        out[name] = jnp.asarray(drawn.astype(out[name].dtype))
    for name, factor in factors.items():
        out[name] = (out[name] * factor).astype(out[name].dtype)
    return out
```

```python
from contextlib import ExitStack

import concourse.bass as bass
from concourse import mybir

F32 = mybir.dt.float32
F32R = mybir.dt.float32r
I32 = mybir.dt.int32
ALU = mybir.AluOpType
ACT = mybir.ActivationFunctionType
AX_X = mybir.AxisListType.X

P = 128
BANK = 512
HEADS = 8
DH = 64
EPS = 1e-5
ZERO_POINT = 128.0
UT = 2


def build_program(nc, x, ctx_in, wq, wk, wv, wo, bo, gamma, beta, q1, s1, b1, q2, s2, b2, out):
    B, S, D = x.shape
    J, DC = ctx_in.shape[1:]
    INNER = wq.shape[1]
    F = q1.shape[1]
    NT = B * S // P
    NU = NT // UT
    LAST = NU - 1
    UB = NU // B
    C = D // P
    K = INNER // P
    M = F // P
    HJ = HEADS * J
    HALF = HJ // 2
    PAIR = 2 * J
    JC = -(-HJ // P)
    BIAS_ROW = HJ - (JC - 1) * P
    BJ = B * J
    W = UT * P
    assert HEADS * DH == INNER and D == 2 * P and DC - P <= DH and HALF <= BANK and 0 < BIAS_ROW < P
    chunk0 = [k * PAIR // P for k in range(K)]
    assert all((k + 1) * PAIR <= (chunk0[k] + 2) * P for k in range(K))
    assert s1.shape[0] == C and s2.shape[0] == M

    x_v = x.rearrange("b s c -> (b s) c").rearrange("(n p) c -> p n c", p=P)
    out_v = out.rearrange("b s c -> (b s) c").rearrange("(n p) c -> p n c", p=P)
    ctx_v = ctx_in.rearrange("b j c -> (b j) c")

    with ExitStack() as stack:
        def sb(name, shape, dt=F32):
            return stack.enter_context(nc.sbuf_tensor(name, shape, dt))

        def psum(name):
            return stack.enter_context(nc.psum_tensor(name, [P, BANK], F32))

        def sem(name):
            return stack.enter_context(nc.semaphore(name))

        x_sb = sb("x_sb", [P, NT, D])
        ctx_a = sb("ctx_a", [P, DC])
        ctx_b = sb("ctx_b", [BJ - P, DC])
        wq_sb = sb("wq_sb", [P, C, INNER])
        wk_a, wk_b = sb("wk_a", [P, INNER]), sb("wk_b", [DC - P, INNER])
        wv_a, wv_b = sb("wv_a", [P, INNER]), sb("wv_b", [DC - P, INNER])
        wo_sb = sb("wo_sb", [P, K, D])
        bo_sb = sb("bo_sb", [1, D])
        vec_rows = sb("vec_rows", [2 * C + M, P])
        vec_cols = sb("vec_cols", [P, 2 * C + M])
        gamma_sb, beta_sb, b1_sb = vec_cols[:, 0:C], vec_cols[:, C:2 * C], vec_cols[:, 2 * C:2 * C + M]
        b2_sb = sb("b2_sb", [P, D])
        q1_sb = sb("q1_sb", [P, C, F], I32)
        q2_sb = sb("q2_sb", [P, M, D], I32)
        w1_sb = sb("w1_sb", [P, C, F])
        w2_sb = sb("w2_sb", [P, M, D])
        ident = sb("ident", [P, P])
        bias_hot = sb("bias_hot", [1, P])
        neg_half = sb("neg_half", [P, NT])
        ctxT_a, ctxT_b = sb("ctxT_a", [P, BJ]), sb("ctxT_b", [DC - P, BJ])
        kT = sb("kT", [P, K, B, PAIR])
        vT = sb("vT", [P, K, B, 2 * P])
        wqT = sb("wqT", [P, K, D])
        m_hi, m_lo = sb("m_hi", [P, B, C, 2, HALF], F32R), sb("m_lo", [P, B, C, 2, HALF], F32R)
        vw_hi, vw_lo = sb("vw_hi", [P, B * JC, D], F32R), sb("vw_lo", [P, B * JC, D], F32R)
        w1_hi, w1_lo = sb("w1_hi", [P, C, F], F32R), sb("w1_lo", [P, C, F], F32R)
        w2_hi, w2_lo = sb("w2_hi", [P, M, D], F32R), sb("w2_lo", [P, M, D], F32R)
        b1_eff = sb("b1_eff", [P, M])
        b2_half = sb("b2_half", [P, D])
        bn1 = sb("bn1", [P, NT, 6])
        mv1 = sb("mv1", [P, NT, 2])
        veps1, rstd1 = sb("veps1", [P, NT]), sb("rstd1", [P, NT])
        xn = sb("xn", [P, UT, D])
        xT_hi, xT_lo = sb("xT_hi", [P, C, W], F32R), sb("xT_lo", [P, C, W], F32R)
        probs = sb("probs", [P, UT, JC * P])
        smax, ssum, rsum = sb("smax", [P, UT, HEADS]), sb("ssum", [P, UT, HEADS]), sb("rsum", [P, UT, HEADS])
        pT_hi, pT_lo = sb("pT_hi", [P, UT, JC, P], F32R), sb("pT_lo", [P, UT, JC, P], F32R)
        bn2 = sb("bn2", [P, UT, 6])
        mv2 = sb("mv2", [P, UT, 2])
        vars2 = sb("vars2", [P, 2, UT])
        rstd2 = sb("rstd2", [P, 2, UT])
        ln, hn = sb("ln", [P, UT, D]), sb("hn", [P, UT, D])
        hT_hi, hT_lo = sb("hT_hi", [P, C, W], F32R), sb("hT_lo", [P, C, W], F32R)
        y = q1_sb[:, :, :].bitcast(F32).rearrange("p c (m w) -> p (c m) w", w=W)
        y_hi, y_lo = sb("y_hi", [P, M, W], F32R), sb("y_lo", [P, M, W], F32R)

        work = [stack.enter_context(nc.psum_tensor(f"work{i}", [P, 2 * BANK], F32)) for i in range(2)]
        hid = [psum(f"hid{i}") for i in range(2)]
        tok = [psum(f"tok{i}") for i in range(2)]
        prep_ring = hid + tok

        def f32(t):
            return t.bitcast(F32)

        ctx_in_sem, wk_in, wv_in, wq_in, wo_in = sem("ctx_in"), sem("wk_in"), sem("wv_in"), sem("wq_in"), sem("wo_in")
        x_first_in, x_rest_in = sem("x_first_in"), sem("x_rest_in")
        vec_in, q1_in, q2_in = sem("vec_in"), sem("q1_in"), sem("q2_in")
        stored = sem("stored")
        zeroed, const_ready, vT_zeroed = sem("zeroed"), sem("const_ready"), sem("vT_zeroed")
        prep_filled, prep_hi_done, prep_freed = sem("prep_filled"), sem("prep_hi_done"), sem("prep_freed")
        bn1_done, mv1_done, veps1_done, rstd1_done = sem("bn1_done"), sem("mv1_done"), sem("veps1_done"), sem("rstd1_done")
        w1_done, w1_hi_done, w1_split = sem("w1_done"), sem("w1_hi_done"), sem("w1_split")
        w2_done, w2_hi_done, w2_split = sem("w2_done"), sem("w2_hi_done"), sem("w2_split")
        b2_done = sem("b2_done")
        work_filled = sem("work_filled")
        work_hi_done = sem("work_hi_done")
        work_freed = sem("work_freed")
        xn_done, max_done, exp_done = sem("xn_done"), sem("max_done"), sem("exp_done")
        sum_done, rsum_done, norm_done = sem("sum_done"), sem("rsum_done"), sem("norm_done")
        tok_filled, tok_freed = sem("tok_filled"), sem("tok_freed")
        bn2_done, mv2_done, vars2_done, rstd2_done = sem("bn2_done"), sem("mv2_done"), sem("vars2_done"), sem("rstd2_done")
        hn_done, res_part, res_done = sem("hn_done"), sem("res_part"), sem("res_done")
        hid_filled, silu_done, y_hi_done, y_lo_done = sem("hid_filled"), sem("silu_done"), sem("y_hi_done"), sem("y_lo_done")

        def wait_alone(engine, semaphore, count):
            engine.wait_ge(semaphore, 1)
            engine.wait_ge(semaphore, count)

        USES, HIS = 6, 4

        def score_use(a, j, first=False):
            return 1 + j if first else a * USES + 2 * j

        def h_use(f, last=False):
            return LAST * USES + 5 if last else f * USES + USES + 1

        def x_use(a, first=False):
            return 0 if first else a * USES - 3

        def prob_use(a, j, last=False):
            return a * USES + 4 + j - int(last)

        def h_his(f, last=False):
            return (LAST + 1) * HIS if last else f * HIS + HIS + 1

        def x_his(a, first=False):
            return 1 if first else a * HIS - 2

        def prob_his(a, j, last=False):
            return a * HIS + 3 + j - int(last)

        def att_use(a, j, first=False):
            return j if first else a * 4 - 2 + j

        def fc2_use(f, j, last=False):
            return LAST * 4 + 2 + j if last else f * 4 + 4 + j

        HP = M // 2

        VEC_AT, H0 = BJ, BANK // 2
        assert VEC_AT + 2 * C + M <= H0

        K_AT, WQ_AT, M_AT = 1, 1 + K, 3 + K
        V_AT = M_AT + 2 * C
        VW_AT = V_AT + K
        M1_AT = VW_AT + B * JC // 2
        B1_AT = M1_AT + 2 * C
        assert B == 2 and B * JC % 2 == 0 and K == 4

        with nc.Block() as block:

            @block.sync
            def _(sp):
                sp.dma_start(ctx_a[:, :], ctx_v[0:P, :]).then_inc(ctx_in_sem, 16)
                sp.dma_start(ctx_b[:, :], ctx_v[P:BJ, :]).then_inc(ctx_in_sem, 16)
                sp.dma_start(wk_a[:, :], wk[0:P, :]).then_inc(wk_in, 16)
                sp.dma_start(wk_b[:, :], wk[P:DC, :]).then_inc(wk_in, 16)
                sp.dma_start(wq_sb[:, :, :], wq.rearrange("(n p) f -> p n f", p=P)).then_inc(wq_in, 16)
                sp.dma_start(wv_a[:, :], wv[0:P, :]).then_inc(wv_in, 16)
                sp.dma_start(wv_b[:, :], wv[P:DC, :]).then_inc(wv_in, 16)
                sp.dma_start(wo_sb[:, :, :], wo.rearrange("(n p) f -> p n f", p=P)).then_inc(wo_in, 16)
                sp.dma_start(q1_sb[:, :, :], q1.rearrange("(n p) f -> p n f", p=P)).then_inc(q1_in, 16)
                for c in range(C):
                    sp.dma_start(w1_sb[:, c, :], s1[c:c + 1, :].to_broadcast([P, F])).then_inc(q1_in, 16)
                sp.dma_start(x_sb[:, UT:NT, :], x_v[:, UT:NT, :]).then_inc(x_rest_in, 16)
                sp.dma_start(q2_sb[:, :, :], q2.rearrange("(n p) f -> p n f", p=P)).then_inc(q2_in, 16)
                sp.dma_start(w2_sb[:, :, :], s2.rearrange("(o m) e -> o m e", o=1).to_broadcast([P, M, D])).then_inc(q2_in, 16)

                def store(f, last=False):
                    for j in range(UT):
                        sp.wait_ge(tok_freed, fc2_use(f, j, last) + 1)
                        t = f * UT + j
                        sp.dma_start(out_v[:, bass.ds(t, 1), :], x_sb[:, bass.ds(t, 1), :]).then_inc(stored, 16)

                with sp.Fori(0, LAST) as f:
                    store(f)
                store(LAST, last=True)
                sp.wait_ge(stored, 16 * NT)

            @block.gpsimd
            def _(pool):
                nc.gpsimd.memset(ident[:, :], 0.0).then_inc(zeroed, 1)
                nc.gpsimd.memset(kT[:, :, :, :], 0.0).then_inc(zeroed, 1)
                nc.gpsimd.memset(bias_hot[:, :], 0.0).then_inc(zeroed, 1)
                nc.gpsimd.memset(probs[:, :, HJ:JC * P], 0.0).then_inc(zeroed, 1)
                nc.gpsimd.memset(neg_half[:, :], -0.5).then_inc(zeroed, 1)
                pool.wait_ge(zeroed, 5)
                nc.gpsimd.affine_select(out=ident[:, :], in_=ident[:, :], compare_op=ALU.not_equal, fill=1.0,
                                        base=0, pattern=[[-1, P]], channel_multiplier=1).then_inc(const_ready, 1)
                nc.gpsimd.memset(bias_hot[:, BIAS_ROW:BIAS_ROW + 1], 1.0).then_inc(const_ready, 1)
                nc.gpsimd.memset(probs[:, :, HJ:HJ + 1], 1.0).then_inc(const_ready, 1)

                def rsqrt1(n, t0, t1):
                    pool.wait_ge(mv1_done, t1)
                    nc.gpsimd.tensor_scalar(veps1[:, t0:t1], mv1[:, t0:t1, 1], EPS, None, ALU.add).then_inc(veps1_done, 1)
                    pool.wait_ge(veps1_done, n)
                    nc.gpsimd.tensor_tensor(rstd1[:, t0:t1], veps1[:, t0:t1], neg_half[:, t0:t1],
                                            ALU.pow).then_inc(rstd1_done, 1)

                rsqrt1(1, 0, UT)
                nc.gpsimd.memset(vT[:, :, :, :], 0.0).then_inc(vT_zeroed, 1)
                pool.wait_ge(vec_in, 16 * 5)
                nc.gpsimd.tensor_scalar(b2_half[:, :], b2_sb[:, :], 0.5, None, ALU.mult).then_inc(b2_done, 1)
                rsqrt1(2, UT, NT)

                def normalize(a):
                    for j in range(UT):
                        wait_alone(pool, rsum_done, a * UT + j + 1)
                        p = probs[:, j, 0:HJ].rearrange("p (h j) -> p h j", h=HEADS)
                        nc.gpsimd.tensor_tensor(p, p, rsum[:, j, :].unsqueeze(2).to_broadcast([P, HEADS, J]),
                                                ALU.mult).then_inc(norm_done, 1)

                def rsqrt2(a):
                    wait_alone(pool, mv2_done, a * UT + UT)
                    nc.gpsimd.tensor_scalar(vars2[:, 0, :], mv2[:, :, 1], EPS, None, ALU.add).then_inc(vars2_done, 1)
                    nc.gpsimd.tensor_scalar(vars2[:, 1, :], mv2[:, :, 1], 1.0 + EPS, EPS * EPS,
                                            ALU.mult, ALU.add).then_inc(vars2_done, 1)
                    wait_alone(pool, vars2_done, a * 2 + 2)
                    nc.gpsimd.tensor_tensor(rstd2[:, :, :].rearrange("p a b -> p (a b)"),
                                            vars2[:, :, :].rearrange("p a b -> p (a b)"),
                                            neg_half[:, 0:2 * UT], ALU.pow).then_inc(rstd2_done, 1)

                def residual(f):
                    wait_alone(pool, hn_done, f * UT + UT)
                    r = x_sb[:, bass.ds(f * UT, UT), :]
                    nc.gpsimd.tensor_tensor(r, r, ln[:, :, :], ALU.add).then_inc(res_part, 1)
                    wait_alone(pool, res_part, f + 1)
                    nc.gpsimd.tensor_tensor(r, r, b2_half[:, :].unsqueeze(1).to_broadcast([P, UT, D]),
                                            ALU.add).then_inc(res_done, 1)

                def lower_y(f):
                    for p in range(HP):
                        pool.wait_ge(y_hi_done, f * HP + p + 1)
                        two = slice(2 * p, 2 * p + 2)
                        nc.gpsimd.tensor_tensor(y_lo[:, two, :], y[:, two, :], f32(y_hi[:, two, :]),
                                                ALU.subtract).then_inc(y_lo_done, 1)

                normalize(0)
                pool.wait_ge(w2_hi_done, 1)
                nc.gpsimd.tensor_tensor(w2_lo[:, :, :], w2_sb[:, :, :], f32(w2_hi[:, :, :]),
                                        ALU.subtract).then_inc(w2_split, 1)
                pool.wait_ge(b2_done, 1)
                rsqrt2(0)
                with pool.Fori(1, NU) as a:
                    residual(a - 1)
                    normalize(a)
                    lower_y(a - 1)
                    rsqrt2(a)
                residual(LAST)
                lower_y(LAST)

            @block.scalar
            def _(act):
                act.dma_start(x_sb[:, 0:UT, :], x_v[:, 0:UT, :]).then_inc(x_first_in, 16)
                act.dma_start(vec_rows[0:C, :], gamma.rearrange("(n p) -> n p", p=P)).then_inc(vec_in, 16)
                act.dma_start(vec_rows[C:2 * C, :], beta.rearrange("(n p) -> n p", p=P)).then_inc(vec_in, 16)
                act.dma_start(vec_rows[2 * C:2 * C + M, :], b1.rearrange("(n p) -> n p", p=P)).then_inc(vec_in, 16)
                act.dma_start(b2_sb[:, :], b2.rearrange("(o e) -> o e", o=1).to_broadcast([P, D])).then_inc(vec_in, 16)
                act.dma_start(bo_sb[:, :], bo.rearrange("(o e) -> o e", o=1)).then_inc(vec_in, 16)

                def prep_hi(use, dst, src, scale):
                    act.wait_ge(prep_filled, use + 1)
                    nc.scalar.activation(dst, src, ACT.Copy, scale=scale).then_inc(prep_hi_done, 1)

                def m_hi_parts(b, at):
                    for n in range(2 * C):
                        c, h = n // 2, n % 2
                        prep_hi(at + n, m_hi[:, b, c, h, :], prep_ring[(at + n) % 4][:, 0:HALF], DH ** -0.5)

                def exponentials(a, j, first=False):
                    act.wait_ge(work_freed, score_use(a, j, first) + 1)
                    nc.scalar.activation(probs[:, j, 0:HJ], probs[:, j, 0:HJ], ACT.Exp).then_inc(exp_done, 1)

                def work_hi(use, slot, dst, width):
                    act.wait_ge(work_filled, use + 1)
                    nc.scalar.activation(dst, work[slot][:, 0:width], ACT.Copy).then_inc(work_hi_done, 1)

                def flat(t):
                    return t.rearrange("p a b -> p (a b)")

                def prob_hi(a, j, slot, last=False):
                    work_hi(prob_use(a, j, last), slot, flat(pT_hi[:, j, :, :]), JC * P)

                def hidden(f, first, between):
                    for p in range(HP):
                        act.wait_ge(hid_filled, f * HP + p + 1)
                        if not first:
                            act.wait_ge(y_lo_done, f * HP + p + 1 - HP)
                        for q in range(2):
                            m = 2 * p + q
                            last = nc.scalar.activation(y[:, m, :], hid[p % 2][:, q * W:(q + 1) * W], ACT.Silu,
                                                        bias=b1_eff[:, m:m + 1])
                        last.then_inc(silu_done, 1)
                        act.wait_ge(silu_done, f * HP + p + 1)
                        nc.scalar.activation(y_hi[:, 2 * p:2 * p + 2, :], y[:, 2 * p:2 * p + 2, :],
                                             ACT.Copy).then_inc(y_hi_done, 1)
                        if p in between:
                            between[p]()

                m_hi_parts(0, M_AT)
                work_hi(x_use(0, True), 0, flat(xT_hi[:, :, :]), C * W)
                exponentials(0, 0, True)
                exponentials(0, 1, True)
                for n in range(B * JC // 2):
                    prep_hi(VW_AT + n, vw_hi[:, 2 * n:2 * n + 2, :], prep_ring[(VW_AT + n) % 4][:, :], 1.0)
                m_hi_parts(1, M1_AT)
                work_hi(x_use(1), 1, flat(xT_hi[:, :, :]), C * W)
                act.wait_ge(w1_done, 1)
                for c in range(C):
                    nc.scalar.activation(w1_hi[:, c, :], w1_sb[:, c, :], ACT.Copy,
                                         scale=gamma_sb[:, c:c + 1]).then_inc(w1_hi_done, 1)
                prob_hi(0, 0, 0)
                prob_hi(0, 1, 1)
                act.wait_ge(w2_done, 1)
                nc.scalar.activation(w2_hi[:, :, :], w2_sb[:, :, :], ACT.Copy).then_inc(w2_hi_done, 1)
                act.wait_ge(prep_freed, B1_AT + 1)

                def step(a, first, last):
                    exponentials(a, 0)
                    work_hi(h_use(a - 1), 1, flat(hT_hi[:, :, :]), C * W)
                    exponentials(a, 1)
                    if not last:
                        work_hi(x_use(a + 1), 1, flat(xT_hi[:, :, :]), C * W)
                    hidden(a - 1, first, {2: lambda: prob_hi(a, 0, int(last), last),
                                          3: lambda: prob_hi(a, 1, 1 - int(last), last)})

                step(1, True, False)
                with act.Fori(2, LAST) as a:
                    step(a, False, False)
                step(LAST, False, True)
                work_hi(h_use(LAST, True), 1, flat(hT_hi[:, :, :]), C * W)
                hidden(LAST, False, {})

            @block.vector
            def _(dve):
                def stats1(t):
                    nc.vector.bn_stats(bn1[:, t, :], x_sb[:, t, :]).then_inc(bn1_done, 1)
                    dve.wait_ge(bn1_done, t + 1)
                    nc.vector.bn_aggr(mv1[:, t, :], bn1[:, t, :]).then_inc(mv1_done, 1)

                def normalize_x(a):
                    for j in range(UT):
                        t = a * UT + j
                        ins = nc.vector.tensor_scalar(xn[:, j, :], x_sb[:, bass.ds(t, 1), :], mv1[:, bass.ds(t, 1), 0],
                                                      rstd1[:, bass.ds(t, 1)], ALU.subtract, ALU.mult)
                    ins.then_inc(xn_done, 1)

                def prep_wait(use):
                    dve.wait_ge(prep_filled, use + 1)
                    return prep_ring[use % 4]

                def m_lo_parts(b, at):
                    for n in range(2 * C):
                        c, h = n // 2, n % 2
                        dve.wait_ge(prep_hi_done, (0 if b == 0 else 2 * C + B * JC // 2) + n + 1)
                        nc.vector.scalar_tensor_tensor(m_lo[:, b, c, h, :], prep_ring[(at + n) % 4][:, 0:HALF], DH ** -0.5,
                                                       f32(m_hi[:, b, c, h, :]), ALU.mult,
                                                       ALU.subtract).then_inc(prep_freed, 1)

                def flat(t):
                    return t.rearrange("p a b -> p (a b)")

                def work_lo(his, slot, dst, hi, width):
                    dve.wait_ge(work_hi_done, his)
                    nc.vector.tensor_tensor(dst, work[slot][:, 0:width], f32(hi), ALU.subtract).then_inc(work_freed, 1)

                def shift_scores(a, j, slot, first=False):
                    dve.wait_ge(work_filled, score_use(a, j, first) + 1)
                    s = work[slot][:, :].rearrange("p (n c) -> p n c", n=2)[:, :, 0:HALF].rearrange("p n (h j) -> p n h j", j=J)
                    mx = smax[:, j, :].rearrange("p (n h) -> p n h", n=2)
                    nc.vector.tensor_reduce(mx, s, AX_X, ALU.max).then_inc(max_done, 1)
                    dve.wait_ge(max_done, a * UT + j + 1)
                    nc.vector.tensor_tensor(probs[:, j, 0:HJ].rearrange("p (n h j) -> p n h j", n=2, j=J), s,
                                            mx.unsqueeze(3).to_broadcast([P, 2, HEADS // 2, J]),
                                            ALU.subtract).then_inc(work_freed, 1)

                def invert_sums(a, j):
                    dve.wait_ge(exp_done, a * UT + j + 1)
                    nc.vector.tensor_reduce(ssum[:, j, :], probs[:, j, 0:HJ].rearrange("p (h j) -> p h j", h=HEADS),
                                            AX_X, ALU.add).then_inc(sum_done, 1)
                    dve.wait_ge(sum_done, a * UT + j + 1)
                    nc.vector.reciprocal(rsum[:, j, :], ssum[:, j, :]).then_inc(rsum_done, 1)

                def prob_lo(a, j, slot, last=False):
                    work_lo(prob_his(a, j, last), slot, flat(pT_lo[:, j, :, :]), flat(pT_hi[:, j, :, :]), JC * P)

                def add_attention(a, j, first=False):
                    use = att_use(a, j, first)
                    x2 = x_sb[:, bass.ds(a * UT + j, 1), :]
                    dve.wait_ge(tok_filled, use + 1)
                    nc.vector.tensor_tensor(x2, tok[j][:, 0:D].unsqueeze(1), x2, ALU.add).then_inc(tok_freed, 1)
                    wait_alone(dve, tok_freed, use + 1)
                    nc.vector.bn_stats(bn2[:, j, :], x2).then_inc(bn2_done, 1)
                    wait_alone(dve, bn2_done, a * UT + j + 1)
                    nc.vector.bn_aggr(mv2[:, j, :], bn2[:, j, :]).then_inc(mv2_done, 1)

                def normalize_x2(a):
                    dve.wait_ge(rstd2_done, a + 1)
                    for n, dst in ((1, hn), (0, ln)):
                        for j in range(UT):
                            ins = nc.vector.tensor_scalar(dst[:, j, :].unsqueeze(1), x_sb[:, bass.ds(a * UT + j, 1), :],
                                                          mv2[:, j, 0:1], rstd2[:, n, j:j + 1], ALU.subtract, ALU.mult)
                            ins.then_inc(hn_done, 1) if n == 0 else None

                def finish_tile(f, j, last=False):
                    dve.wait_ge(tok_filled, fc2_use(f, j, last) + 1)
                    dve.wait_ge(res_done, f + 1)
                    o = x_sb[:, bass.ds(f * UT + j, 1), :]
                    nc.vector.scalar_tensor_tensor(o, tok[j][:, 0:D].unsqueeze(1), 0.5, o, ALU.mult,
                                                   ALU.add).then_inc(tok_freed, 1)

                dve.wait_ge(x_first_in, 16)
                for t in range(UT):
                    stats1(t)
                r = prep_wait(0)
                nc.vector.tensor_copy(ctxT_a[:, :], r[:, 0:BJ])
                nc.vector.tensor_copy(vec_cols[:, :], r[:, VEC_AT:VEC_AT + 2 * C + M])
                nc.vector.tensor_copy(ctxT_b[:, :], r[0:DC - P, H0:H0 + BJ]).then_inc(prep_freed, 1)
                dve.wait_ge(zeroed, 5)
                for k in range(K):
                    r = prep_wait(K_AT + k)[:, 0:BJ].rearrange("p (b j) -> p b j", b=B)
                    nc.vector.tensor_copy(kT[0:DH, k, :, 0:J], r[0:DH, :, :])
                    nc.vector.tensor_copy(kT[DH:P, k, :, J:PAIR], r[DH:P, :, :]).then_inc(prep_freed, 1)
                for n in range(2):
                    r = prep_wait(WQ_AT + n)
                    nc.vector.tensor_copy(wqT[:, 2 * n:2 * n + 2, :],
                                          r[:, :].rearrange("p (k e) -> p k e", k=2)).then_inc(prep_freed, 1)
                dve.wait_ge(mv1_done, UT)
                dve.wait_ge(rstd1_done, 1)
                normalize_x(0)
                m_lo_parts(0, M_AT)
                work_lo(x_his(0, True), 0, flat(xT_lo[:, :, :]), flat(xT_hi[:, :, :]), C * W)
                shift_scores(0, 0, 1, True)
                shift_scores(0, 1, 0, True)
                dve.wait_ge(vT_zeroed, 1)
                for k in range(K):
                    r = prep_wait(V_AT + k)[:, 0:BJ].rearrange("p (b j) -> p b j", b=B)
                    at = k * PAIR - chunk0[k] * P
                    nc.vector.tensor_copy(vT[0:DH, k, :, at:at + J], r[0:DH, :, :])
                    nc.vector.tensor_copy(vT[DH:P, k, :, at + J:at + PAIR], r[DH:P, :, :]).then_inc(prep_freed, 1)
                invert_sums(0, 0)
                invert_sums(0, 1)
                for n in range(B * JC // 2):
                    dve.wait_ge(prep_hi_done, 2 * C + n + 1)
                    nc.vector.tensor_tensor(vw_lo[:, 2 * n:2 * n + 2, :],
                                            prep_ring[(VW_AT + n) % 4][:, :].rearrange("p (m e) -> p m e", m=2),
                                            f32(vw_hi[:, 2 * n:2 * n + 2, :]), ALU.subtract).then_inc(prep_freed, 1)
                m_lo_parts(1, M1_AT)
                dve.wait_ge(x_rest_in, 16)
                for t in range(UT, NT):
                    stats1(t)
                dve.wait_ge(q1_in, 16 * (1 + C))
                nc.vector.scalar_tensor_tensor(w1_sb[:, :, :], q1_sb[:, :, :], -ZERO_POINT, w1_sb[:, :, :],
                                               ALU.add, ALU.mult).then_inc(w1_done, 1)
                dve.wait_ge(mv1_done, NT)
                dve.wait_ge(rstd1_done, 2)
                dve.wait_ge(work_filled, x_use(0, True) + 1)
                normalize_x(1)
                work_lo(x_his(1), 1, flat(xT_lo[:, :, :]), flat(xT_hi[:, :, :]), C * W)
                dve.wait_ge(q2_in, 16 * 2)
                nc.vector.scalar_tensor_tensor(w2_sb[:, :, :], q2_sb[:, :, :], -ZERO_POINT, w2_sb[:, :, :],
                                               ALU.add, ALU.mult).then_inc(w2_done, 1)
                prob_lo(0, 0, 0)
                prob_lo(0, 1, 1)
                add_attention(0, 0, True)
                add_attention(0, 1, True)
                r = prep_wait(B1_AT)
                nc.vector.tensor_tensor(b1_eff[:, :], r[:, 0:M], b1_sb[:, :], ALU.add).then_inc(prep_freed, 1)
                for c in range(C):
                    dve.wait_ge(w1_hi_done, c + 1)
                    nc.vector.scalar_tensor_tensor(w1_lo[:, c, :], w1_sb[:, c, :], gamma_sb[:, c:c + 1],
                                                   f32(w1_hi[:, c, :]), ALU.mult, ALU.subtract).then_inc(w1_split, 1)
                normalize_x2(0)

                def step(a, last):
                    shift_scores(a, 0, 0)
                    work_lo(h_his(a - 1), 1, flat(hT_lo[:, :, :]), flat(hT_hi[:, :, :]), C * W)
                    if not last:
                        normalize_x(a + 1)
                    shift_scores(a, 1, 0)
                    invert_sums(a, 0)
                    invert_sums(a, 1)
                    if not last:
                        work_lo(x_his(a + 1), 1, flat(xT_lo[:, :, :]), flat(xT_hi[:, :, :]), C * W)
                    prob_lo(a, 0, int(last), last)
                    prob_lo(a, 1, 1 - int(last), last)
                    add_attention(a, 0)
                    add_attention(a, 1)
                    finish_tile(a - 1, 0)
                    normalize_x2(a)
                    finish_tile(a - 1, 1)

                with dve.Fori(1, LAST) as a:
                    step(a, False)
                step(LAST, True)
                work_lo(h_his(LAST, True), 1, flat(hT_lo[:, :, :]), flat(hT_hi[:, :, :]), C * W)
                finish_tile(LAST, 0, True)
                finish_tile(LAST, 1, True)

            @block.tensor
            def _(pe):
                mm = nc.tensor.matmul

                def transposes(slot, src, use, wait_free=True):
                    if wait_free:
                        pe.wait_ge(work_freed, use - 1)
                    for j in range(UT):
                        for c in range(C):
                            ins = nc.tensor.transpose(work[slot][:, c * W + j * P:c * W + (j + 1) * P],
                                                      src[:, j, c * P:(c + 1) * P], ident[:, :])
                    ins.then_inc(work_filled, 1)

                def scores(a, j, slot, b, first=False):
                    use = score_use(a, j, first)
                    pe.wait_ge(work_freed, use - 1)
                    pe.wait_ge(work_freed, x_use(a, first) + 1)
                    for h in range(2):
                        o = work[slot][:, h * BANK:h * BANK + HALF]
                        steps = [(xt, m, c) for c in range(C) for xt, m in ((xT_hi, m_hi), (xT_hi, m_lo), (xT_lo, m_hi))]
                        for n, (xt, m, c) in enumerate(steps):
                            ins = mm(o, xt[:, c, j * P:(j + 1) * P], m[:, b, c, h, :], start=n == 0, stop=n == len(steps) - 1)
                    ins.then_inc(work_filled, 1)

                def prob_transposes(a, j, slot, last=False):
                    pe.wait_ge(norm_done, a * UT + j + 1)
                    pe.wait_ge(work_freed, prob_use(a, j, last) - 1)
                    for m in range(JC):
                        ins = nc.tensor.transpose(work[slot][:, m * P:(m + 1) * P], probs[:, j, m * P:(m + 1) * P], ident[:, :])
                    ins.then_inc(work_filled, 1)

                def attention_out(a, j, b, first=False, last=False):
                    use = att_use(a, j, first)
                    if not first:
                        pe.wait_ge(tok_freed, use - 1)
                    pe.wait_ge(work_freed, prob_use(a, j, last) + 1)
                    steps = [(p, v, m) for m in range(JC) for p, v in ((pT_hi, vw_hi), (pT_hi, vw_lo), (pT_lo, vw_hi))]
                    for n, (p, v, m) in enumerate(steps):
                        ins = mm(tok[j][:, 0:D], p[:, j, m, :], v[:, b * JC + m, :], start=n == 0, stop=n == len(steps) - 1)
                    ins.then_inc(tok_filled, 1)

                def fc1_pair(f, p, first=False, last=False):
                    if p == 0:
                        pe.wait_ge(work_freed, h_use(f, last) + 1)
                    if not (first and p < 2):
                        pe.wait_ge(silu_done, f * HP + p - 1)
                    steps = [(w, h, c) for c in range(C) for w, h in ((w1_hi, hT_hi), (w1_hi, hT_lo), (w1_lo, hT_hi))]
                    for q in range(2):
                        m = 2 * p + q
                        for n, (w, h, c) in enumerate(steps):
                            ins = mm(hid[p % 2][:, q * W:(q + 1) * W], w[:, c, m * P:(m + 1) * P], h[:, c, :],
                                     start=n == 0, stop=n == len(steps) - 1)
                    ins.then_inc(hid_filled, 1)

                def fc2(f, j, last=False):
                    pe.wait_ge(tok_freed, fc2_use(f, j, last) - 1)
                    n = 0
                    for m in range(M):
                        if j == 0 and m % 2 == 0:
                            pe.wait_ge(y_lo_done, f * HP + m // 2 + 1)
                        for s, w in ((y_hi, w2_hi), (y_hi, w2_lo), (y_lo, w2_hi)):
                            ins = mm(tok[j][:, 0:D], s[:, m, j * P:(j + 1) * P], w[:, m, :], start=n == 0, stop=n == 3 * M - 1)
                            n += 1
                    ins.then_inc(tok_filled, 1)

                def prep_bank(use):
                    if use >= 4:
                        pe.wait_ge(prep_freed, use - 3)
                    return prep_ring[use % 4]

                def project(at, wa, wb):
                    for k in range(K):
                        r = prep_bank(at + k)
                        mm(r[:, 0:BJ], wa[:, k * P:(k + 1) * P], ctxT_a[:, :], start=True, stop=False)
                        mm(r[:, 0:BJ], wb[:, k * P:(k + 1) * P], ctxT_b[:, :], start=False, stop=True).then_inc(prep_filled, 1)

                def make_m(b, at):
                    for n in range(2 * C):
                        c, h = n // 2, n % 2
                        r = prep_bank(at + n)
                        for q in range(2):
                            k = 2 * h + q
                            ins = mm(r[:, q * PAIR:(q + 1) * PAIR], wqT[:, k, c * P:(c + 1) * P], kT[:, k, b, :],
                                     start=True, stop=True)
                        ins.then_inc(prep_filled, 1)

                pe.wait_ge(const_ready, 3)
                pe.wait_ge(ctx_in_sem, 32)
                r = prep_bank(0)
                NV = 2 * C + M
                pe.wait_ge(vec_in, 16 * 5)
                nc.tensor.transpose(r[:, VEC_AT:VEC_AT + NV], vec_rows[:, :], ident[0:NV, 0:NV])
                nc.tensor.transpose(r[:, 0:P], ctx_a[:, 0:P], ident[:, :])
                nc.tensor.transpose(r[:, P:BJ], ctx_b[:, 0:P], ident[0:BJ - P, 0:BJ - P])
                nc.tensor.transpose(r[0:DC - P, H0:H0 + P], ctx_a[:, P:DC], ident[:, :])
                nc.tensor.transpose(r[0:DC - P, H0 + P:H0 + BJ], ctx_b[:, P:DC],
                                    ident[0:BJ - P, 0:BJ - P]).then_inc(prep_filled, 1)
                pe.wait_ge(wk_in, 32)
                pe.wait_ge(prep_freed, 1)
                project(K_AT, wk_a, wk_b)
                pe.wait_ge(wq_in, 16)
                for n in range(2):
                    r = prep_bank(WQ_AT + n)
                    for q in range(2):
                        for c in range(C):
                            k = 2 * n + q
                            ins = nc.tensor.transpose(r[:, q * D + c * P:q * D + (c + 1) * P],
                                                      wq_sb[:, c, k * P:(k + 1) * P], ident[:, :])
                    ins.then_inc(prep_filled, 1)
                pe.wait_ge(prep_freed, M_AT)
                make_m(0, M_AT)
                pe.wait_ge(xn_done, 1)
                transposes(0, xn, x_use(0, True), wait_free=False)
                pe.wait_ge(prep_freed, V_AT)
                pe.wait_ge(work_freed, x_use(0, True) + 1)
                scores(0, 0, 1, 0, True)
                scores(0, 1, 0, 0, True)
                pe.wait_ge(wv_in, 32)
                project(V_AT, wv_a, wv_b)
                pe.wait_ge(wo_in, 16)
                pe.wait_ge(prep_freed, VW_AT)
                for n in range(B * JC // 2):
                    r = prep_bank(VW_AT + n)
                    for q in range(2):
                        b, m = divmod(2 * n + q, JC)
                        o = r[:, q * D:(q + 1) * D]
                        ks = [k for k in range(K) if k * PAIR < (m + 1) * P and (k + 1) * PAIR > m * P]
                        assert all(0 <= m - chunk0[k] < 2 for k in ks)
                        for k in ks:
                            n0 = (m - chunk0[k]) * P
                            ins = mm(o, vT[:, k, b, n0:n0 + P], wo_sb[:, k, :], start=k == ks[0],
                                     stop=k == ks[-1] and m < JC - 1)
                        if m == JC - 1:
                            ins = mm(o, bias_hot[0:1, :], bo_sb[0:1, :], start=False, stop=True)
                    ins.then_inc(prep_filled, 1)
                make_m(1, M1_AT)
                pe.wait_ge(xn_done, 2)
                transposes(1, xn, x_use(1))
                pe.wait_ge(w1_done, 1)
                r = prep_bank(B1_AT)
                for m in range(M):
                    for c in range(C):
                        ins = mm(r[:, m:m + 1], w1_sb[:, c, m * P:(m + 1) * P], beta_sb[:, c:c + 1],
                                 start=c == 0, stop=c == C - 1)
                ins.then_inc(prep_filled, 1)
                prob_transposes(0, 0, 0)
                prob_transposes(0, 1, 1)
                pe.wait_ge(prep_freed, B1_AT)
                attention_out(0, 0, 0, first=True)
                attention_out(0, 1, 0, first=True)
                pe.wait_ge(prep_freed, B1_AT + 1)
                pe.wait_ge(w1_split, C)

                def step(a, b, first=False, last=False):
                    scores(a, 0, 0, b)
                    pe.wait_ge(hn_done, a * UT)
                    transposes(1, hn, h_use(a - 1))
                    scores(a, 1, 0, b)
                    if not last:
                        pe.wait_ge(xn_done, a + 2)
                        transposes(1, xn, x_use(a + 1))
                    for p in range(HP):
                        if p == HP - 1:
                            prob_transposes(a, 0, int(last), last)
                        fc1_pair(a - 1, p, first)
                    prob_transposes(a, 1, 1 - int(last), last)
                    if first:
                        pe.wait_ge(w2_split, 1)
                    attention_out(a, 0, b, last=last)
                    attention_out(a, 1, b, last=last)
                    fc2(a - 1, 0)
                    fc2(a - 1, 1)

                step(1, 0, first=True)
                with pe.Fori(2, UB) as a:
                    step(a, 0)
                with pe.Fori(UB, LAST) as a:
                    step(a, 1)
                step(LAST, 1, last=True)
                pe.wait_ge(hn_done, NT)
                transposes(1, hn, h_use(LAST, True))
                for p in range(HP):
                    fc1_pair(LAST, p, last=True)
                fc2(LAST, 0, True)
                fc2(LAST, 1, True)


_INS = ["x", "ctx_768", "L0_xattn_Wq", "L0_xattn_Wk", "L0_xattn_Wv", "L0_xattn_Wo", "L0_xattn_bo",
        "L0_ffn_ln_gamma", "L0_ffn_ln_beta", "L0_ffn_fc1_q", "L0_ffn_fc1_scales", "L0_ffn_fc1_bias",
        "L0_ffn_fc2_q", "L0_ffn_fc2_scales", "L0_ffn_fc2_bias"]


def kernel(**inputs):
    import numpy as _np
    import concourse.bacc as _bacc
    from concourse import mybir as _mybir
    from concourse.bass_utils import run_bass_kernel_spmd as _run

    nc = _bacc.Bacc("TRN2", target_bir_lowering=False, num_devices=1)
    arrays, args = {}, []
    for name in _INS:
        a = _np.ascontiguousarray(inputs[name])
        arrays[f"in_{name}"] = a
        args.append(nc.dram_tensor(f"in_{name}", a.shape, _mybir.dt.from_np(a.dtype), kind="ExternalInput").ap())
    shape = tuple(inputs["x"].shape)
    args.append(nc.dram_tensor("out_x", shape, _mybir.dt.float32, kind="ExternalOutput").ap())
    build_program(nc, *args)
    r = _run(nc, [arrays], core_ids=[0])
    return r.results[0]["out_x"]
```

```python
from contextlib import ExitStack

import concourse.bass as bass
from concourse import mybir

F32 = mybir.dt.float32
F32R = mybir.dt.float32r
I32 = mybir.dt.int32
ALU = mybir.AluOpType
ACT = mybir.ActivationFunctionType
AX_X = mybir.AxisListType.X

P = 128
BANK = 512
HEADS = 8
DH = 64
EPS = 1e-5
ZERO_POINT = 128.0
UT = 2


def build_program(nc, x, ctx_in, wq, wk, wv, wo, bo, gamma, beta, q1, s1, b1, q2, s2, b2, out):
    B, S, D = x.shape
    J, DC = ctx_in.shape[1:]
    INNER = wq.shape[1]
    F = q1.shape[1]
    NT = B * S // P
    NU = NT // UT
    LAST = NU - 1
    UB = NU // B
    C = D // P
    K = INNER // P
    M = F // P
    HJ = HEADS * J
    HALF = HJ // 2
    PAIR = 2 * J
    JC = -(-HJ // P)
    BIAS_ROW = HJ - (JC - 1) * P
    BJ = B * J
    W = UT * P
    assert HEADS * DH == INNER and D == 2 * P and DC - P <= DH and HALF <= BANK and 0 < BIAS_ROW < P
    chunk0 = [k * PAIR // P for k in range(K)]
    assert all((k + 1) * PAIR <= (chunk0[k] + 2) * P for k in range(K))
    assert s1.shape[0] == C and s2.shape[0] == M

    x_v = x.rearrange("b s c -> (b s) c").rearrange("(n p) c -> p n c", p=P)
    out_v = out.rearrange("b s c -> (b s) c").rearrange("(n p) c -> p n c", p=P)
    ctx_v = ctx_in.rearrange("b j c -> (b j) c")

    with ExitStack() as stack:
        def sb(name, shape, dt=F32):
            return stack.enter_context(nc.sbuf_tensor(name, shape, dt))

        def psum(name):
            return stack.enter_context(nc.psum_tensor(name, [P, BANK], F32))

        def sem(name):
            return stack.enter_context(nc.semaphore(name))

        x_sb = sb("x_sb", [P, NT, D])
        ctx_a = sb("ctx_a", [P, DC])
        ctx_b = sb("ctx_b", [BJ - P, DC])
        wq_sb = sb("wq_sb", [P, C, INNER])
        wk_a, wk_b = sb("wk_a", [P, INNER]), sb("wk_b", [DC - P, INNER])
        wv_a, wv_b = sb("wv_a", [P, INNER]), sb("wv_b", [DC - P, INNER])
        wo_sb = sb("wo_sb", [P, K, D])
        bo_sb = sb("bo_sb", [1, D])
        vec_rows = sb("vec_rows", [2 * C + M, P])
        vec_cols = sb("vec_cols", [P, 2 * C + M])
        gamma_sb, beta_sb, b1_sb = vec_cols[:, 0:C], vec_cols[:, C:2 * C], vec_cols[:, 2 * C:2 * C + M]
        b2_sb = sb("b2_sb", [P, D])
        q1_sb = sb("q1_sb", [P, C, F], I32)
        q2_sb = sb("q2_sb", [P, M, D], I32)
        w1_sb = sb("w1_sb", [P, C, F])
        w2_sb = sb("w2_sb", [P, M, D])
        ident = sb("ident", [P, P])
        bias_hot = sb("bias_hot", [1, P])
        neg_half = sb("neg_half", [P, NT])
        table_probe = sb("table_probe", [P, 1])
        ctxT_a, ctxT_b = sb("ctxT_a", [P, BJ]), sb("ctxT_b", [DC - P, BJ])
        kT = sb("kT", [P, K, B, PAIR])
        vT = sb("vT", [P, K, B, 2 * P])
        wqT = sb("wqT", [P, K, D])
        m_hi, m_lo = sb("m_hi", [P, B, C, 2, HALF], F32R), sb("m_lo", [P, B, C, 2, HALF], F32R)
        vw_hi, vw_lo = sb("vw_hi", [P, B * JC, D], F32R), sb("vw_lo", [P, B * JC, D], F32R)
        w1_hi, w1_lo = sb("w1_hi", [P, C, F], F32R), sb("w1_lo", [P, C, F], F32R)
        w2_hi, w2_lo = sb("w2_hi", [P, M, D], F32R), sb("w2_lo", [P, M, D], F32R)
        b1_eff = sb("b1_eff", [P, M])
        b2_half = sb("b2_half", [P, D])
        bn1 = sb("bn1", [P, NT, 6])
        mv1 = sb("mv1", [P, NT, 2])
        veps1, rstd1 = sb("veps1", [P, NT]), sb("rstd1", [P, NT])
        xn = sb("xn", [P, UT, D])
        xT_hi, xT_lo = sb("xT_hi", [P, C, W], F32R), sb("xT_lo", [P, C, W], F32R)
        probs = sb("probs", [P, UT, JC * P])
        smax, ssum, rsum = sb("smax", [P, UT, HEADS]), sb("ssum", [P, UT, HEADS]), sb("rsum", [P, UT, HEADS])
        pT_hi, pT_lo = sb("pT_hi", [P, UT, JC, P], F32R), sb("pT_lo", [P, UT, JC, P], F32R)
        bn2 = sb("bn2", [P, UT, 6])
        mv2 = sb("mv2", [P, UT, 2])
        vars2 = sb("vars2", [P, 2, UT])
        rstd2 = sb("rstd2", [P, 2, UT])
        ln, hn = sb("ln", [P, UT, D]), sb("hn", [P, UT, D])
        hT_hi, hT_lo = sb("hT_hi", [P, C, W], F32R), sb("hT_lo", [P, C, W], F32R)
        y = q1_sb[:, :, :].bitcast(F32).rearrange("p c (m w) -> p (c m) w", w=W)
        y_hi, y_lo = sb("y_hi", [P, M, W], F32R), sb("y_lo", [P, M, W], F32R)

        work = [stack.enter_context(nc.psum_tensor(f"work{i}", [P, 2 * BANK], F32)) for i in range(2)]
        hid = [psum(f"hid{i}") for i in range(2)]
        tok = [psum(f"tok{i}") for i in range(2)]

        def f32(t):
            return t.bitcast(F32)

        ctx_in_sem, wk_in, wv_in, wq_in, wo_in = sem("ctx_in"), sem("wk_in"), sem("wv_in"), sem("wq_in"), sem("wo_in")
        x0_in, x1_in, x_rest_in = sem("x0_in"), sem("x1_in"), sem("x_rest_in")
        vec_in, b2_in, bo_in, q1_in, q2_in = sem("vec_in"), sem("b2_in"), sem("bo_in"), sem("q1_in"), sem("q2_in")
        stored = sem("stored")
        zeroed, const_ready, vT_zeroed = sem("zeroed"), sem("const_ready"), sem("vT_zeroed")
        prep_filled, prep_hi_done, prep_freed = sem("prep_filled"), sem("prep_hi_done"), sem("prep_freed")
        bn1_done, mv1_done, veps1_done, rstd1_done = sem("bn1_done"), sem("mv1_done"), sem("veps1_done"), sem("rstd1_done")
        w1_done, w1_hi_done, w1_split = sem("w1_done"), sem("w1_hi_done"), sem("w1_split")
        w2_shifted, w2_done, w2_hi_done, w2_split = sem("w2_shifted"), sem("w2_done"), sem("w2_hi_done"), sem("w2_split")
        b2_done = sem("b2_done")
        work_filled = sem("work_filled")
        work_hi_done = sem("work_hi_done")
        work_freed = sem("work_freed")
        xn_done, max_done, exp_done = sem("xn_done"), sem("max_done"), sem("exp_done")
        sum_done, rsum_done, norm_done = sem("sum_done"), sem("rsum_done"), sem("norm_done")
        tok_filled, tok_freed = sem("tok_filled"), sem("tok_freed")
        bn2_done, mv2_done, vars2_done, rstd2_done = sem("bn2_done"), sem("mv2_done"), sem("vars2_done"), sem("rstd2_done")
        hn_done, res_part, res_done = sem("hn_done"), sem("res_part"), sem("res_done")
        hid_filled, silu_done, y_hi_done, y_lo_done = sem("hid_filled"), sem("silu_done"), sem("y_hi_done"), sem("y_lo_done")

        def wait_alone(engine, semaphore, count):
            engine.wait_ge(semaphore, 1)
            engine.wait_ge(semaphore, count)

        def first_unit(a):
            return isinstance(a, int) and a == 0

        def score_use(a, j):
            return 6 * a + j + int(first_unit(a))

        def prob_use(a, j):
            return 6 * a + 3 + j

        def x_use(a):
            return 0 if first_unit(a) else 6 * a - 1

        def h_use(a, last=False):
            return 6 * a + (5 if last else 8)

        PROB_SLOT, X_SLOT, H_SLOT = (1, 0), 1, 0

        def score_slot(a, j):
            return 1 - j if first_unit(a) else j

        def prob_his(a, j):
            return 4 * a + 2 + j

        def x_his(a):
            return 1 if first_unit(a) else 4 * a

        def h_his(a, last=False):
            return 4 * a + 5 - int(last)

        def att_use(a, j):
            return j if first_unit(a) else 4 * a - 2 + j

        def fc2_use(f, j, last=False):
            return 4 * f + 4 + j - 2 * int(last)

        HP = M // 2

        H0 = BANK // 2
        K_AT, WQ_AT = 1, 1 + K
        VEC_AT = WQ_AT + 2
        M0_AT = VEC_AT + 1
        V_AT = M0_AT + 2 * C
        M1_AT = V_AT + K
        VW_AT = M1_AT + 2 * C
        B1_AT = VW_AT + B * JC // 2
        assert B == 2 and B * JC % 2 == 0 and K == 4
        assert B1_AT % 4 < 2

        def prep_bank(use):
            return (hid + tok)[use % 4]

        with nc.Block() as block:

            @block.sync
            def _(sp):
                sp.dma_start(ctx_a[:, :], ctx_v[0:P, :]).then_inc(ctx_in_sem, 16)
                sp.dma_start(ctx_b[:, :], ctx_v[P:BJ, :]).then_inc(ctx_in_sem, 16)
                sp.dma_start(wk_a[:, :], wk[0:P, :]).then_inc(wk_in, 16)
                sp.dma_start(wk_b[:, :], wk[P:DC, :]).then_inc(wk_in, 16)
                sp.dma_start(wq_sb[:, :, :], wq.rearrange("(n p) f -> p n f", p=P)).then_inc(wq_in, 16)
                sp.dma_start(wv_a[:, :], wv[0:P, :]).then_inc(wv_in, 16)
                sp.dma_start(wv_b[:, :], wv[P:DC, :]).then_inc(wv_in, 16)
                sp.dma_start(wo_sb[:, :, :], wo.rearrange("(n p) f -> p n f", p=P)).then_inc(wo_in, 16)
                sp.dma_start(q1_sb[:, :, :], q1.rearrange("(n p) f -> p n f", p=P)).then_inc(q1_in, 16)
                for c in range(C):
                    sp.dma_start(w1_sb[:, c, :], s1[c:c + 1, :].to_broadcast([P, F])).then_inc(q1_in, 16)
                sp.dma_start(q2_sb[:, :, :], q2.rearrange("(n p) f -> p n f", p=P)).then_inc(q2_in, 16)
                sp.dma_start(w2_sb[:, :, :], s2.rearrange("(o m) e -> o m e", o=1).to_broadcast([P, M, D])).then_inc(q2_in, 16)
                sp.dma_start(x_sb[:, 2 * UT:NT, :], x_v[:, 2 * UT:NT, :]).then_inc(x_rest_in, 16)

                def store(f, last=False):
                    for j in range(UT):
                        sp.wait_ge(tok_freed, fc2_use(f, j, last) + 1)
                        t = f * UT + j
                        sp.dma_start(out_v[:, bass.ds(t, 1), :], x_sb[:, bass.ds(t, 1), :]).then_inc(stored, 16)

                with sp.Fori(0, LAST) as f:
                    store(f)
                store(LAST, last=True)
                sp.wait_ge(stored, 16 * NT)

            @block.gpsimd
            def _(pool):
                nc.gpsimd.memset(ident[:, :], 0.0).then_inc(zeroed, 1)
                pool.wait_ge(zeroed, 1)
                nc.gpsimd.affine_select(out=ident[:, :], in_=ident[:, :], compare_op=ALU.not_equal, fill=1.0,
                                        base=0, pattern=[[-1, P]], channel_multiplier=1).then_inc(const_ready, 1)
                nc.gpsimd.memset(neg_half[:, :], -0.5).then_inc(const_ready, 1)
                nc.gpsimd.memset(kT[:, :, :, :], 0.0).then_inc(zeroed, 1)
                nc.gpsimd.memset(bias_hot[:, :], 0.0).then_inc(zeroed, 1)
                nc.gpsimd.memset(probs[:, :, HJ:JC * P], 0.0).then_inc(zeroed, 1)
                pool.wait_ge(zeroed, 4)
                nc.gpsimd.memset(bias_hot[:, BIAS_ROW:BIAS_ROW + 1], 1.0).then_inc(const_ready, 1)
                nc.gpsimd.memset(probs[:, :, HJ:HJ + 1], 1.0).then_inc(const_ready, 1)
                pool.wait_ge(const_ready, 4)

                def rsqrt1(n, t0, t1):
                    pool.wait_ge(mv1_done, t1)
                    nc.gpsimd.tensor_scalar(veps1[:, t0:t1], mv1[:, t0:t1, 1], EPS, None, ALU.add).then_inc(veps1_done, 1)
                    pool.wait_ge(veps1_done, n)
                    nc.gpsimd.tensor_tensor(rstd1[:, t0:t1], veps1[:, t0:t1], neg_half[:, t0:t1],
                                            ALU.pow).then_inc(rstd1_done, 1)

                rsqrt1(1, 0, UT)
                nc.gpsimd.memset(vT[:, :, :, :], 0.0).then_inc(vT_zeroed, 1)
                pool.wait_ge(b2_in, 16)
                nc.gpsimd.tensor_scalar(b2_half[:, :], b2_sb[:, :], 0.5, None, ALU.mult).then_inc(b2_done, 1)
                rsqrt1(2, UT, 2 * UT)

                def normalize(a):
                    for j in range(UT):
                        wait_alone(pool, rsum_done, a * UT + j + 1)
                        p = probs[:, j, 0:HJ].rearrange("p (h j) -> p h j", h=HEADS)
                        nc.gpsimd.tensor_tensor(p, p, rsum[:, j, :].unsqueeze(2).to_broadcast([P, HEADS, J]),
                                                ALU.mult).then_inc(norm_done, 1)

                def rsqrt2(a):
                    wait_alone(pool, mv2_done, a * UT + UT)
                    nc.gpsimd.tensor_scalar(vars2[:, 0, :], mv2[:, :, 1], EPS, None, ALU.add).then_inc(vars2_done, 1)
                    nc.gpsimd.tensor_scalar(vars2[:, 1, :], mv2[:, :, 1], 1.0 + EPS, EPS * EPS,
                                            ALU.mult, ALU.add).then_inc(vars2_done, 1)
                    wait_alone(pool, vars2_done, a * 2 + 2)
                    nc.gpsimd.tensor_tensor(rstd2[:, :, :].rearrange("p a b -> p (a b)"),
                                            vars2[:, :, :].rearrange("p a b -> p (a b)"),
                                            neg_half[:, 0:2 * UT], ALU.pow).then_inc(rstd2_done, 1)

                def residual(f):
                    wait_alone(pool, hn_done, f * UT + UT)
                    r = x_sb[:, bass.ds(f * UT, UT), :]
                    nc.gpsimd.tensor_tensor(r, r, ln[:, :, :], ALU.add).then_inc(res_part, 1)
                    wait_alone(pool, res_part, f + 1)
                    nc.gpsimd.tensor_tensor(r, r, b2_half[:, :].unsqueeze(1).to_broadcast([P, UT, D]),
                                            ALU.add).then_inc(res_done, 1)

                def lower_y(f):
                    for p in range(HP):
                        pool.wait_ge(y_hi_done, f * HP + p + 1)
                        two = slice(2 * p, 2 * p + 2)
                        nc.gpsimd.tensor_tensor(y_lo[:, two, :], y[:, two, :], f32(y_hi[:, two, :]),
                                                ALU.subtract).then_inc(y_lo_done, 1)

                normalize(0)
                pool.wait_ge(w2_shifted, 1)
                pool.wait_ge(q2_in, 16 * 2)
                nc.gpsimd.tensor_tensor(w2_sb[:, :, :], f32(q2_sb[:, :, :]), w2_sb[:, :, :], ALU.mult).then_inc(w2_done, 1)
                rsqrt1(3, 2 * UT, 3 * UT)
                pool.wait_ge(b2_done, 1)
                rsqrt2(0)
                pool.wait_ge(w2_hi_done, 1)
                nc.gpsimd.tensor_tensor(w2_lo[:, :, :], w2_sb[:, :, :], f32(w2_hi[:, :, :]),
                                        ALU.subtract).then_inc(w2_split, 1)

                def step(a):
                    residual(a - 1)
                    normalize(a)
                    lower_y(a - 1)
                    rsqrt2(a)

                residual(0)
                normalize(1)
                rsqrt1(4, 3 * UT, NT)
                lower_y(0)
                rsqrt2(1)
                with pool.Fori(2, NU) as a:
                    step(a)
                residual(LAST)

            @block.scalar
            def _(act):
                act.dma_start(x_sb[:, 0:UT, :], x_v[:, 0:UT, :]).then_inc(x0_in, 16)
                act.dma_start(x_sb[:, UT:2 * UT, :], x_v[:, UT:2 * UT, :]).then_inc(x1_in, 16)
                act.dma_start(vec_rows[0:C, :], gamma.rearrange("(n p) -> n p", p=P)).then_inc(vec_in, 16)
                act.dma_start(vec_rows[C:2 * C, :], beta.rearrange("(n p) -> n p", p=P)).then_inc(vec_in, 16)
                act.dma_start(vec_rows[2 * C:2 * C + M, :], b1.rearrange("(n p) -> n p", p=P)).then_inc(vec_in, 16)
                act.dma_start(bo_sb[:, :], bo.rearrange("(o e) -> o e", o=1)).then_inc(bo_in, 16)
                act.dma_start(b2_sb[:, :], b2.rearrange("(o e) -> o e", o=1).to_broadcast([P, D])).then_inc(b2_in, 16)

                def prep_hi(use, dst, src, scale):
                    act.wait_ge(prep_filled, use + 1)
                    nc.scalar.activation(dst, src, ACT.Copy, scale=scale).then_inc(prep_hi_done, 1)

                def m_hi_parts(b, at):
                    for n in range(2 * C):
                        c, h = n // 2, n % 2
                        prep_hi(at + n, m_hi[:, b, c, h, :], prep_bank(at + n)[:, 0:HALF], DH ** -0.5)

                def exponentials(a, j):
                    act.wait_ge(work_freed, score_use(a, j) + 1)
                    nc.scalar.activation(probs[:, j, 0:HJ], probs[:, j, 0:HJ], ACT.Exp).then_inc(exp_done, 1)

                def work_hi(use, slot, dst, width):
                    act.wait_ge(work_filled, use + 1)
                    nc.scalar.activation(dst, work[slot][:, 0:width], ACT.Copy).then_inc(work_hi_done, 1)

                def flat(t):
                    return t.rearrange("p a b -> p (a b)")

                def x_hi(a, slot=X_SLOT):
                    work_hi(x_use(a), slot, flat(xT_hi[:, :, :]), C * W)

                def h_hi(a, slot=H_SLOT, last=False):
                    work_hi(h_use(a, last), slot, flat(hT_hi[:, :, :]), C * W)

                def prob_hi(a, j):
                    work_hi(prob_use(a, j), PROB_SLOT[j], flat(pT_hi[:, j, :, :]), JC * P)

                def hidden(f, p, first=False):
                    act.wait_ge(hid_filled, f * HP + p + 1)
                    if not first:
                        act.wait_ge(y_lo_done, f * HP + p + 1 - HP)
                    for q in range(2):
                        m = 2 * p + q
                        last = nc.scalar.activation(y[:, m, :], hid[p % 2][:, q * W:(q + 1) * W], ACT.Silu,
                                                    bias=b1_eff[:, m:m + 1])
                    last.then_inc(silu_done, 1)
                    act.wait_ge(silu_done, f * HP + p + 1)
                    nc.scalar.activation(y_hi[:, 2 * p:2 * p + 2, :], y[:, 2 * p:2 * p + 2, :],
                                         ACT.Copy).then_inc(y_hi_done, 1)

                act.wait_ge(const_ready, 2)
                m_hi_parts(0, M0_AT)
                x_hi(0, slot=0)
                exponentials(0, 0)
                exponentials(0, 1)
                m_hi_parts(1, M1_AT)
                act.wait_ge(q2_in, 16 * 2)
                nc.scalar.activation(f32(q2_sb[:, :, :]), q2_sb[:, :, :], ACT.Copy, bias=-ZERO_POINT).then_inc(w2_shifted, 1)
                for n in range(B * JC // 2):
                    prep_hi(VW_AT + n, vw_hi[:, 2 * n:2 * n + 2, :], prep_bank(VW_AT + n)[:, :], 1.0)
                    if n < C:
                        act.wait_ge(w1_done, 1)
                        nc.scalar.activation(w1_hi[:, n, :], w1_sb[:, n, :], ACT.Copy,
                                             scale=gamma_sb[:, n:n + 1]).then_inc(w1_hi_done, 1)
                prob_hi(0, 0)
                prob_hi(0, 1)
                x_hi(1)
                act.wait_ge(w2_done, 1)
                nc.scalar.activation(w2_hi[:, :, :], w2_sb[:, :, :], ACT.Copy).then_inc(w2_hi_done, 1)

                def step(a, first=False, last=False):
                    exponentials(a, 0)
                    h_hi(a - 1)
                    exponentials(a, 1)
                    nc.scalar.activation(table_probe[:, :], neg_half[:, 0:1], ACT.Silu)
                    if first:
                        act.wait_ge(prep_freed, B1_AT + 1)
                    hidden(a - 1, 0, first)
                    hidden(a - 1, 1, first)
                    prob_hi(a, 0)
                    prob_hi(a, 1)
                    hidden(a - 1, 2, first)
                    hidden(a - 1, 3, first)
                    if not last:
                        x_hi(a + 1)

                step(1, first=True)
                with act.Fori(2, LAST) as a:
                    step(a)
                step(LAST, last=True)
                h_hi(LAST, slot=1, last=True)
                for p in range(HP):
                    hidden(LAST, p)

            @block.vector
            def _(dve):
                def stats1(t):
                    nc.vector.bn_stats(bn1[:, t, :], x_sb[:, t, :]).then_inc(bn1_done, 1)
                    dve.wait_ge(bn1_done, t + 1)
                    nc.vector.bn_aggr(mv1[:, t, :], bn1[:, t, :]).then_inc(mv1_done, 1)

                def normalize_x(a):
                    for j in range(UT):
                        t = a * UT + j
                        ins = nc.vector.tensor_scalar(xn[:, j, :], x_sb[:, bass.ds(t, 1), :], mv1[:, bass.ds(t, 1), 0],
                                                      rstd1[:, bass.ds(t, 1)], ALU.subtract, ALU.mult)
                    ins.then_inc(xn_done, 1)

                def prep_wait(use):
                    dve.wait_ge(prep_filled, use + 1)
                    return prep_bank(use)

                def m_lo_parts(b, at):
                    for n in range(2 * C):
                        c, h = n // 2, n % 2
                        dve.wait_ge(prep_hi_done, b * 2 * C + n + 1)
                        nc.vector.scalar_tensor_tensor(m_lo[:, b, c, h, :], prep_bank(at + n)[:, 0:HALF], DH ** -0.5,
                                                       f32(m_hi[:, b, c, h, :]), ALU.mult,
                                                       ALU.subtract).then_inc(prep_freed, 1)

                def flat(t):
                    return t.rearrange("p a b -> p (a b)")

                def work_lo(his, slot, dst, hi, width):
                    dve.wait_ge(work_hi_done, his)
                    nc.vector.tensor_tensor(dst, work[slot][:, 0:width], f32(hi), ALU.subtract).then_inc(work_freed, 1)

                def shift_scores(a, j):
                    dve.wait_ge(work_filled, score_use(a, j) + 1)
                    s = work[score_slot(a, j)][:, :].rearrange("p (n c) -> p n c", n=2)[:, :, 0:HALF].rearrange("p n (h j) -> p n h j", j=J)
                    mx = smax[:, j, :].rearrange("p (n h) -> p n h", n=2)
                    nc.vector.tensor_reduce(mx, s, AX_X, ALU.max).then_inc(max_done, 1)
                    dve.wait_ge(max_done, a * UT + j + 1)
                    nc.vector.tensor_tensor(probs[:, j, 0:HJ].rearrange("p (n h j) -> p n h j", n=2, j=J), s,
                                            mx.unsqueeze(3).to_broadcast([P, 2, HEADS // 2, J]),
                                            ALU.subtract).then_inc(work_freed, 1)

                def invert_sums(a, j):
                    dve.wait_ge(exp_done, a * UT + j + 1)
                    nc.vector.tensor_reduce(ssum[:, j, :], probs[:, j, 0:HJ].rearrange("p (h j) -> p h j", h=HEADS),
                                            AX_X, ALU.add).then_inc(sum_done, 1)
                    dve.wait_ge(sum_done, a * UT + j + 1)
                    nc.vector.reciprocal(rsum[:, j, :], ssum[:, j, :]).then_inc(rsum_done, 1)

                def x_lo(a, slot=X_SLOT):
                    work_lo(x_his(a), slot, flat(xT_lo[:, :, :]), flat(xT_hi[:, :, :]), C * W)

                def h_lo(a, slot=H_SLOT, last=False):
                    work_lo(h_his(a, last), slot, flat(hT_lo[:, :, :]), flat(hT_hi[:, :, :]), C * W)

                def prob_lo(a, j):
                    work_lo(prob_his(a, j), PROB_SLOT[j], flat(pT_lo[:, j, :, :]), flat(pT_hi[:, j, :, :]), JC * P)

                def add_attention(a, j):
                    use = att_use(a, j)
                    x2 = x_sb[:, bass.ds(a * UT + j, 1), :]
                    dve.wait_ge(tok_filled, use + 1)
                    nc.vector.tensor_tensor(x2, tok[j][:, 0:D].unsqueeze(1), x2, ALU.add).then_inc(tok_freed, 1)
                    wait_alone(dve, tok_freed, use + 1)
                    nc.vector.bn_stats(bn2[:, j, :], x2).then_inc(bn2_done, 1)
                    wait_alone(dve, bn2_done, a * UT + j + 1)
                    nc.vector.bn_aggr(mv2[:, j, :], bn2[:, j, :]).then_inc(mv2_done, 1)

                def normalize_x2(a, first=False):
                    dve.wait_ge(rstd2_done, a + 1)
                    if not first:
                        dve.wait_ge(res_done, a)
                    for n, dst in ((1, hn), (0, ln)):
                        for j in range(UT):
                            ins = nc.vector.tensor_scalar(dst[:, j, :].unsqueeze(1), x_sb[:, bass.ds(a * UT + j, 1), :],
                                                          mv2[:, j, 0:1], rstd2[:, n, j:j + 1], ALU.subtract, ALU.mult)
                            ins.then_inc(hn_done, 1) if n == 0 else None

                def finish_tile(f, j, last=False):
                    dve.wait_ge(tok_filled, fc2_use(f, j, last) + 1)
                    dve.wait_ge(res_done, f + 1)
                    o = x_sb[:, bass.ds(f * UT + j, 1), :]
                    nc.vector.scalar_tensor_tensor(o, tok[j][:, 0:D].unsqueeze(1), 0.5, o, ALU.mult,
                                                   ALU.add).then_inc(tok_freed, 1)

                dve.wait_ge(x0_in, 16)
                for t in range(UT):
                    stats1(t)
                r = prep_wait(0)
                nc.vector.tensor_copy(ctxT_a[:, :], r[:, 0:BJ])
                nc.vector.tensor_copy(ctxT_b[:, :], r[0:DC - P, H0:H0 + BJ]).then_inc(prep_freed, 1)
                dve.wait_ge(mv1_done, UT)
                dve.wait_ge(rstd1_done, 1)
                normalize_x(0)
                dve.wait_ge(zeroed, 4)
                for k in range(K):
                    r = prep_wait(K_AT + k)[:, 0:BJ].rearrange("p (b j) -> p b j", b=B)
                    nc.vector.tensor_copy(kT[0:DH, k, :, 0:J], r[0:DH, :, :])
                    nc.vector.tensor_copy(kT[DH:P, k, :, J:PAIR], r[DH:P, :, :]).then_inc(prep_freed, 1)
                for n in range(2):
                    r = prep_wait(WQ_AT + n)
                    nc.vector.tensor_copy(wqT[:, 2 * n:2 * n + 2, :],
                                          r[:, :].rearrange("p (k e) -> p k e", k=2)).then_inc(prep_freed, 1)
                nc.vector.tensor_copy(vec_cols[:, :], prep_wait(VEC_AT)[:, 0:2 * C + M]).then_inc(prep_freed, 1)
                m_lo_parts(0, M0_AT)
                x_lo(0, slot=0)
                dve.wait_ge(vT_zeroed, 1)
                for k in range(K):
                    r = prep_wait(V_AT + k)[:, 0:BJ].rearrange("p (b j) -> p b j", b=B)
                    at = k * PAIR - chunk0[k] * P
                    nc.vector.tensor_copy(vT[0:DH, k, :, at:at + J], r[0:DH, :, :])
                    nc.vector.tensor_copy(vT[DH:P, k, :, at + J:at + PAIR], r[DH:P, :, :]).then_inc(prep_freed, 1)
                dve.wait_ge(x1_in, 16)
                for t in range(UT, 2 * UT):
                    stats1(t)
                shift_scores(0, 0)
                shift_scores(0, 1)
                m_lo_parts(1, M1_AT)
                invert_sums(0, 0)
                invert_sums(0, 1)
                dve.wait_ge(q1_in, 16 * (1 + C))
                nc.vector.scalar_tensor_tensor(w1_sb[:, :, :], q1_sb[:, :, :], -ZERO_POINT, w1_sb[:, :, :],
                                               ALU.add, ALU.mult).then_inc(w1_done, 1)
                for n in range(B * JC // 2):
                    dve.wait_ge(prep_hi_done, 4 * C + n + 1)
                    nc.vector.tensor_tensor(vw_lo[:, 2 * n:2 * n + 2, :],
                                            prep_bank(VW_AT + n)[:, :].rearrange("p (m e) -> p m e", m=2),
                                            f32(vw_hi[:, 2 * n:2 * n + 2, :]), ALU.subtract).then_inc(prep_freed, 1)
                    if n == 0:
                        dve.wait_ge(work_filled, x_use(0) + 1)
                        dve.wait_ge(mv1_done, 2 * UT)
                        dve.wait_ge(rstd1_done, 2)
                        normalize_x(1)
                    if 2 <= n < 2 + C:
                        c = n - 2
                        dve.wait_ge(w1_hi_done, c + 1)
                        nc.vector.scalar_tensor_tensor(w1_lo[:, c, :], w1_sb[:, c, :], gamma_sb[:, c:c + 1],
                                                       f32(w1_hi[:, c, :]), ALU.mult, ALU.subtract).then_inc(w1_split, 1)
                prob_lo(0, 0)
                prob_lo(0, 1)
                x_lo(1)
                dve.wait_ge(x_rest_in, 16)
                for t in range(2 * UT, 3 * UT):
                    stats1(t)
                add_attention(0, 0)
                add_attention(0, 1)
                normalize_x2(0, first=True)

                def step(a, first=False, last=False):
                    shift_scores(a, 0)
                    shift_scores(a, 1)
                    h_lo(a - 1)
                    if first:
                        nc.vector.tensor_tensor(b1_eff[:, :], prep_wait(B1_AT)[:, 0:M], b1_sb,
                                                ALU.add).then_inc(prep_freed, 1)
                    invert_sums(a, 0)
                    invert_sums(a, 1)
                    if not first:
                        finish_tile(a - 2, 1)
                    if first:
                        dve.wait_ge(mv1_done, 3 * UT)
                        dve.wait_ge(rstd1_done, 3)
                    if not last:
                        normalize_x(a + 1)
                    if first:
                        for t in range(3 * UT, NT):
                            stats1(t)
                    prob_lo(a, 0)
                    prob_lo(a, 1)
                    add_attention(a, 0)
                    add_attention(a, 1)
                    if not last:
                        x_lo(a + 1)
                    normalize_x2(a)
                    finish_tile(a - 1, 0)

                step(1, first=True)
                dve.wait_ge(mv1_done, NT)
                dve.wait_ge(rstd1_done, 4)
                with dve.Fori(2, LAST) as a:
                    step(a)
                step(LAST, last=True)
                finish_tile(LAST - 1, 1)
                h_lo(LAST, slot=1, last=True)
                for p in range(HP):
                    dve.wait_ge(y_lo_done, LAST * HP + p)
                    dve.wait_ge(y_hi_done, LAST * HP + p + 1)
                    two = slice(2 * p, 2 * p + 2)
                    nc.vector.tensor_tensor(y_lo[:, two, :], y[:, two, :], f32(y_hi[:, two, :]),
                                            ALU.subtract).then_inc(y_lo_done, 1)
                finish_tile(LAST, 0, last=True)
                finish_tile(LAST, 1, last=True)

            @block.tensor
            def _(pe):
                mm = nc.tensor.matmul

                def transposes(slot, src, use):
                    if not (isinstance(use, int) and use < 2):
                        pe.wait_ge(work_freed, use - 1)
                    for j in range(UT):
                        for c in range(C):
                            ins = nc.tensor.transpose(work[slot][:, c * W + j * P:c * W + (j + 1) * P],
                                                      src[:, j, c * P:(c + 1) * P], ident[:, :])
                    ins.then_inc(work_filled, 1)

                def scores(a, j, b):
                    if not (isinstance(a, int) and score_use(a, j) < 2):
                        pe.wait_ge(work_freed, score_use(a, j) - 1)
                    if j == 0:
                        pe.wait_ge(work_freed, x_use(a) + 1)
                    for h in range(2):
                        o = work[score_slot(a, j)][:, h * BANK:h * BANK + HALF]
                        steps = [(xt, m, c) for c in range(C) for xt, m in ((xT_hi, m_hi), (xT_hi, m_lo), (xT_lo, m_hi))]
                        for n, (xt, m, c) in enumerate(steps):
                            ins = mm(o, xt[:, c, j * P:(j + 1) * P], m[:, b, c, h, :], start=n == 0, stop=n == len(steps) - 1)
                    ins.then_inc(work_filled, 1)

                def prob_transposes(a, j):
                    pe.wait_ge(norm_done, a * UT + j + 1)
                    pe.wait_ge(work_freed, prob_use(a, j) - 1)
                    for m in range(JC):
                        ins = nc.tensor.transpose(work[PROB_SLOT[j]][:, m * P:(m + 1) * P], probs[:, j, m * P:(m + 1) * P],
                                                  ident[:, :])
                    ins.then_inc(work_filled, 1)

                def attention_out(a, j, b, first=False):
                    if not first:
                        pe.wait_ge(tok_freed, att_use(a, j) - 1)
                    pe.wait_ge(work_freed, prob_use(a, j) + 1)
                    steps = [(p, v, m) for m in range(JC) for p, v in ((pT_hi, vw_hi), (pT_hi, vw_lo), (pT_lo, vw_hi))]
                    for n, (p, v, m) in enumerate(steps):
                        ins = mm(tok[j][:, 0:D], p[:, j, m, :], v[:, b * JC + m, :], start=n == 0, stop=n == len(steps) - 1)
                    ins.then_inc(tok_filled, 1)

                def fc1_pair(f, p, first=False, last=False):
                    if p == 0:
                        pe.wait_ge(work_freed, h_use(f, last) + 1)
                    if not (first and p < 2):
                        pe.wait_ge(silu_done, f * HP + p - 1)
                    steps = [(w, h, c) for c in range(C) for w, h in ((w1_hi, hT_hi), (w1_hi, hT_lo), (w1_lo, hT_hi))]
                    for q in range(2):
                        m = 2 * p + q
                        for n, (w, h, c) in enumerate(steps):
                            ins = mm(hid[p % 2][:, q * W:(q + 1) * W], w[:, c, m * P:(m + 1) * P], h[:, c, :],
                                     start=n == 0, stop=n == len(steps) - 1)
                    ins.then_inc(hid_filled, 1)

                def fc2(f, j, last=False, midway=None):
                    pe.wait_ge(tok_freed, fc2_use(f, j, last) - 1)
                    n = 0
                    for m in range(M):
                        if m == M // 2 and midway is not None:
                            midway()
                        if j == 0 and m % 2 == 0:
                            pe.wait_ge(y_lo_done, f * HP + m // 2 + 1)
                        for s, w in ((y_hi, w2_hi), (y_hi, w2_lo), (y_lo, w2_hi)):
                            ins = mm(tok[j][:, 0:D], s[:, m, j * P:(j + 1) * P], w[:, m, :], start=n == 0, stop=n == 3 * M - 1)
                            n += 1
                    ins.then_inc(tok_filled, 1)

                def emptied(use):
                    if use >= 4:
                        pe.wait_ge(prep_freed, use - 3)
                    return prep_bank(use)

                def project(at, wa, wb):
                    for k in range(K):
                        r = emptied(at + k)
                        mm(r[:, 0:BJ], wa[:, k * P:(k + 1) * P], ctxT_a[:, :], start=True, stop=False)
                        mm(r[:, 0:BJ], wb[:, k * P:(k + 1) * P], ctxT_b[:, :], start=False, stop=True).then_inc(prep_filled, 1)

                def make_m(b, at):
                    for n in range(2 * C):
                        c, h = n // 2, n % 2
                        r = emptied(at + n)
                        for q in range(2):
                            k = 2 * h + q
                            ins = mm(r[:, q * PAIR:(q + 1) * PAIR], wqT[:, k, c * P:(c + 1) * P], kT[:, k, b, :],
                                     start=True, stop=True)
                        ins.then_inc(prep_filled, 1)

                pe.wait_ge(const_ready, 1)
                pe.wait_ge(ctx_in_sem, 32)
                r = emptied(0)
                nc.tensor.transpose(r[:, 0:P], ctx_a[:, 0:P], ident[:, :])
                nc.tensor.transpose(r[:, P:BJ], ctx_b[:, 0:P], ident[0:BJ - P, 0:BJ - P])
                nc.tensor.transpose(r[0:DC - P, H0:H0 + P], ctx_a[:, P:DC], ident[:, :])
                nc.tensor.transpose(r[0:DC - P, H0 + P:H0 + BJ], ctx_b[:, P:DC],
                                    ident[0:BJ - P, 0:BJ - P]).then_inc(prep_filled, 1)
                pe.wait_ge(wk_in, 32)
                pe.wait_ge(prep_freed, 1)
                project(K_AT, wk_a, wk_b)
                pe.wait_ge(wq_in, 16)
                for n in range(2):
                    r = emptied(WQ_AT + n)
                    for q in range(2):
                        for c in range(C):
                            k = 2 * n + q
                            ins = nc.tensor.transpose(r[:, q * D + c * P:q * D + (c + 1) * P],
                                                      wq_sb[:, c, k * P:(k + 1) * P], ident[:, :])
                    ins.then_inc(prep_filled, 1)
                pe.wait_ge(vec_in, 16 * 3)
                NV = 2 * C + M
                nc.tensor.transpose(emptied(VEC_AT)[:, 0:NV], vec_rows[:, :], ident[0:NV, 0:NV]).then_inc(prep_filled, 1)
                pe.wait_ge(xn_done, 1)
                transposes(0, xn, x_use(0))
                pe.wait_ge(prep_freed, VEC_AT)
                make_m(0, M0_AT)
                pe.wait_ge(wv_in, 32)
                project(V_AT, wv_a, wv_b)
                pe.wait_ge(prep_freed, V_AT)
                scores(0, 0, 0)
                scores(0, 1, 0)
                make_m(1, M1_AT)
                pe.wait_ge(wo_in, 16)
                pe.wait_ge(const_ready, 4)
                pe.wait_ge(bo_in, 16)
                pe.wait_ge(prep_freed, M1_AT)
                for n in range(B * JC // 2):
                    r = emptied(VW_AT + n)
                    for q in range(2):
                        b, m = divmod(2 * n + q, JC)
                        o = r[:, q * D:(q + 1) * D]
                        ks = [k for k in range(K) if k * PAIR < (m + 1) * P and (k + 1) * PAIR > m * P]
                        assert all(0 <= m - chunk0[k] < 2 for k in ks)
                        for k in ks:
                            n0 = (m - chunk0[k]) * P
                            ins = mm(o, vT[:, k, b, n0:n0 + P], wo_sb[:, k, :], start=k == ks[0],
                                     stop=k == ks[-1] and m < JC - 1)
                        if m == JC - 1:
                            ins = mm(o, bias_hot[0:1, :], bo_sb[0:1, :], start=False, stop=True)
                    ins.then_inc(prep_filled, 1)
                prob_transposes(0, 0)
                prob_transposes(0, 1)
                pe.wait_ge(xn_done, 2)
                transposes(X_SLOT, xn, x_use(1))
                pe.wait_ge(prep_freed, B1_AT)
                attention_out(0, 0, 0, first=True)
                attention_out(0, 1, 0, first=True)

                def step(a, b, first=False, last=False):
                    scores(a, 0, b)
                    scores(a, 1, b)
                    pe.wait_ge(hn_done, a * UT)
                    transposes(H_SLOT, hn, h_use(a - 1))
                    if first:
                        pe.wait_ge(w1_done, 1)
                        r = emptied(B1_AT)
                        for m in range(M):
                            for c in range(C):
                                ins = mm(r[:, m:m + 1], w1_sb[:, c, m * P:(m + 1) * P], beta_sb[:, c:c + 1],
                                         start=c == 0, stop=c == C - 1)
                        ins.then_inc(prep_filled, 1)
                        pe.wait_ge(prep_freed, B1_AT + 1)
                        pe.wait_ge(w1_split, C)
                    else:
                        fc2(a - 2, 1)
                    fc1_pair(a - 1, 0, first)
                    fc1_pair(a - 1, 1, first)
                    prob_transposes(a, 0)
                    prob_transposes(a, 1)
                    fc1_pair(a - 1, 2)
                    fc1_pair(a - 1, 3)
                    attention_out(a, 0, b)
                    attention_out(a, 1, b)
                    if not last:
                        pe.wait_ge(xn_done, a + 2)
                        transposes(X_SLOT, xn, x_use(a + 1))
                    if first:
                        pe.wait_ge(w2_split, 1)
                    fc2(a - 1, 0)

                step(1, 0, first=True)
                with pe.Fori(2, UB) as a:
                    step(a, 0)
                with pe.Fori(UB, LAST) as a:
                    step(a, 1)
                step(LAST, 1, last=True)

                def last_h():
                    pe.wait_ge(hn_done, NT)
                    transposes(1 - H_SLOT, hn, h_use(LAST, last=True))

                fc2(LAST - 1, 1, midway=last_h)
                for p in range(HP):
                    fc1_pair(LAST, p, last=True)
                fc2(LAST, 0, last=True)
                fc2(LAST, 1, last=True)


_INS = ["x", "ctx_768", "L0_xattn_Wq", "L0_xattn_Wk", "L0_xattn_Wv", "L0_xattn_Wo", "L0_xattn_bo",
        "L0_ffn_ln_gamma", "L0_ffn_ln_beta", "L0_ffn_fc1_q", "L0_ffn_fc1_scales", "L0_ffn_fc1_bias",
        "L0_ffn_fc2_q", "L0_ffn_fc2_scales", "L0_ffn_fc2_bias"]


def kernel(**inputs):
    import numpy as _np
    import concourse.bacc as _bacc
    from concourse import mybir as _mybir
    from concourse.bass_utils import run_bass_kernel_spmd as _run

    nc = _bacc.Bacc("TRN2", target_bir_lowering=False, num_devices=1)
    arrays, args = {}, []
    for name in _INS:
        a = _np.ascontiguousarray(inputs[name])
        arrays[f"in_{name}"] = a
        args.append(nc.dram_tensor(f"in_{name}", a.shape, _mybir.dt.from_np(a.dtype), kind="ExternalInput").ap())
    shape = tuple(inputs["x"].shape)
    args.append(nc.dram_tensor("out_x", shape, _mybir.dt.float32, kind="ExternalOutput").ap())
    build_program(nc, *args)
    r = _run(nc, [arrays], core_ids=[0])
    return r.results[0]["out_x"]
```

```python
from contextlib import ExitStack

import concourse.bass as bass
from concourse import mybir

F32 = mybir.dt.float32
F32R = mybir.dt.float32r
I32 = mybir.dt.int32
ALU = mybir.AluOpType
ACT = mybir.ActivationFunctionType
AX_X = mybir.AxisListType.X

P = 128
BANK = 512
HEADS = 8
DH = 64
EPS = 1e-5
ZERO_POINT = 128.0
EARLY = 5
WARM = (11, 5)
UT = 2


def build_program(nc, x, ctx_in, wq, wk, wv, wo, bo, gamma, beta, q1, s1, b1, q2, s2, b2, out):
    B, S, D = x.shape
    J, DC = ctx_in.shape[1:]
    INNER = wq.shape[1]
    F = q1.shape[1]
    NT = B * S // P
    NU = NT // UT
    LAST = NU - 1
    UB = NU // B
    C = D // P
    K = INNER // P
    M = F // P
    HJ = HEADS * J
    HALF = HJ // 2
    PAIR = 2 * J
    JC = -(-HJ // P)
    BIAS_ROW = HJ - (JC - 1) * P
    BJ = B * J
    CC = DC // 2
    W = UT * P
    assert HEADS * DH == INNER and D == 2 * P and CC <= P and 2 * BJ <= BANK and HALF <= BANK and 0 < BIAS_ROW < P
    chunk0 = [k * PAIR // P for k in range(K)]
    assert all((k + 1) * PAIR <= (chunk0[k] + 2) * P for k in range(K))
    assert s1.shape[0] == C and s2.shape[0] == M

    x_v = x.rearrange("b s c -> (b s) c").rearrange("(n p) c -> p n c", p=P)
    out_v = out.rearrange("b s c -> (b s) c").rearrange("(n p) c -> p n c", p=P)
    ctx_v = ctx_in.rearrange("b j c -> j b c")

    with ExitStack() as stack:
        def sb(name, shape, dt=F32):
            return stack.enter_context(nc.sbuf_tensor(name, shape, dt))

        def psum(name):
            return stack.enter_context(nc.psum_tensor(name, [P, BANK], F32))

        def sem(name):
            return stack.enter_context(nc.semaphore(name))

        x_sb = sb("x_sb", [P, NT, D])
        ctx_sb = sb("ctx_sb", [J, B, DC])
        wq_sb = sb("wq_sb", [P, C, INNER])
        wk_sb, wv_sb = sb("wk_sb", [CC, 2, INNER]), sb("wv_sb", [CC, 2, INNER])
        wo_sb = sb("wo_sb", [P, K, D])
        bo_sb = sb("bo_sb", [1, D])
        vec_rows = sb("vec_rows", [2 * C + M, P])
        vec_cols = sb("vec_cols", [P, 2 * C + M])
        gamma_sb, beta_sb, b1_sb = vec_cols[:, 0:C], vec_cols[:, C:2 * C], vec_cols[:, 2 * C:2 * C + M]
        b2_sb = sb("b2_sb", [P, D])
        q1_sb = sb("q1_sb", [P, C, F], I32)
        q2_sb = sb("q2_sb", [P, M, D], I32)
        w1_sb = sb("w1_sb", [P, C, F])
        w2_sb = sb("w2_sb", [P, M, D])
        ident = sb("ident", [P, P])
        bias_hot = sb("bias_hot", [1, P])
        neg_half = sb("neg_half", [P, NT])
        table_probe = sb("table_probe", [P, 1])
        ctxT = sb("ctxT", [CC, 2, BJ])
        kT = sb("kT", [P, K, B, PAIR])
        vT = sb("vT", [P, K, B, 2 * P])
        wqT = sb("wqT", [P, K, D])
        m_hi, m_lo = sb("m_hi", [P, B, C, 2, HALF], F32R), sb("m_lo", [P, B, C, 2, HALF], F32R)
        vw_hi, vw_lo = sb("vw_hi", [P, B * JC, D], F32R), sb("vw_lo", [P, B * JC, D], F32R)
        w1_hi, w1_lo = sb("w1_hi", [P, C, F], F32R), sb("w1_lo", [P, C, F], F32R)
        w2_hi, w2_lo = sb("w2_hi", [P, M, D], F32R), sb("w2_lo", [P, M, D], F32R)
        beta_parts = sb("beta_parts", [P, C, 2], F32R)
        b1_part, b1_eff = sb("b1_part", [P, M]), sb("b1_eff", [P, M])
        b2_half = sb("b2_half", [P, D])
        bn1 = sb("bn1", [P, NT, 6])
        mv1 = sb("mv1", [P, NT, 2])
        veps1, rstd1 = sb("veps1", [P, NT]), sb("rstd1", [P, NT])
        xn = sb("xn", [P, UT, D])
        xT_hi, xT_lo = sb("xT_hi", [P, C, W], F32R), sb("xT_lo", [P, C, W], F32R)
        probs = sb("probs", [P, UT, JC * P])
        smax, ssum, rsum = sb("smax", [P, UT, HEADS]), sb("ssum", [P, UT, HEADS]), sb("rsum", [P, UT, HEADS])
        pT_hi, pT_lo = sb("pT_hi", [P, UT, JC, P], F32R), sb("pT_lo", [P, UT, JC, P], F32R)
        bn2 = sb("bn2", [P, UT, 6])
        mv2 = sb("mv2", [P, UT, 2])
        vars2 = sb("vars2", [P, 2, UT])
        rstd2 = sb("rstd2", [P, 2, UT])
        ln, hn = sb("ln", [P, UT, D]), sb("hn", [P, UT, D])
        hT_hi, hT_lo = sb("hT_hi", [P, C, W], F32R), sb("hT_lo", [P, C, W], F32R)
        y = q1_sb[:, :, :].bitcast(F32).rearrange("p c (m w) -> p (c m) w", w=W)
        y_hi, y_lo = sb("y_hi", [P, M, W], F32R), sb("y_lo", [P, M, W], F32R)

        work = [stack.enter_context(nc.psum_tensor(f"work{i}", [P, 2 * BANK], F32)) for i in range(2)]
        hid = [psum(f"hid{i}") for i in range(2)]
        tok = [psum(f"tok{i}") for i in range(2)]

        def f32(t):
            return t.bitcast(F32)

        ctx_in_sem, wk_in, wv_in, wq_in, wo_in = sem("ctx_in"), sem("wk_in"), sem("wv_in"), sem("wq_in"), sem("wo_in")
        x0_in, x1_in, x_rest_in = sem("x0_in"), sem("x1_in"), sem("x_rest_in")
        vec_in, b2_in, bo_in, q1_in = sem("vec_in"), sem("b2_in"), sem("bo_in"), sem("q1_in")
        s1_in, q2_in, s2_in = sem("s1_in"), sem("q2_in"), sem("s2_in")
        stored = sem("stored")
        zeroed, const_ready, vT_zeroed = sem("zeroed"), sem("const_ready"), sem("vT_zeroed")
        prep_filled, prep_hi_done, prep_freed = sem("prep_filled"), sem("prep_hi_done"), sem("prep_freed")
        wqT_done = sem("wqT_done")
        bn1_done, mv1_done, veps1_done, rstd1_done = sem("bn1_done"), sem("mv1_done"), sem("veps1_done"), sem("rstd1_done")
        w1_shifted, beta_hi_done, beta_split = sem("w1_shifted"), sem("beta_hi_done"), sem("beta_split")
        w1_done, w1_hi_done, w1_split = sem("w1_done"), sem("w1_hi_done"), sem("w1_split")
        w2_shifted, w2_done, w2_hi_done, w2_split = sem("w2_shifted"), sem("w2_done"), sem("w2_hi_done"), sem("w2_split")
        b1_part_done, b2_done = sem("b1_part_done"), sem("b2_done")
        work_filled = sem("work_filled")
        work_hi_done = sem("work_hi_done")
        work_freed = sem("work_freed")
        xn_done, max_done, exp_done = sem("xn_done"), sem("max_done"), sem("exp_done")
        sum_done, rsum_done, norm_done = sem("sum_done"), sem("rsum_done"), sem("norm_done")
        tok_filled, tok_freed = sem("tok_filled"), sem("tok_freed")
        bn2_done, mv2_done, vars2_done, rstd2_done = sem("bn2_done"), sem("mv2_done"), sem("vars2_done"), sem("rstd2_done")
        ln_done, hn_done, res_part, res_done = sem("ln_done"), sem("hn_done"), sem("res_part"), sem("res_done")
        hid_filled, silu_done, y_hi_done, y_lo_done = sem("hid_filled"), sem("silu_done"), sem("y_hi_done"), sem("y_lo_done")

        def wait_alone(engine, semaphore, count):
            engine.wait_ge(semaphore, 1)
            engine.wait_ge(semaphore, count)

        def first_unit(a):
            return isinstance(a, int) and a == 0

        def score_use(a, j):
            return 6 * a + j + int(first_unit(a))

        def prob_use(a, j):
            return 6 * a + 3 + j

        def x_use(a):
            return 0 if first_unit(a) else 6 * a - 1

        def h_use(a, last=False):
            return 6 * a + (5 if last else 8)

        PROB_SLOT, X_SLOT, H_SLOT = (1, 0), 1, 0

        def score_slot(a, j):
            return 1 - j if first_unit(a) else j

        def prob_his(a, j):
            return 4 * a + 2 + j

        def x_his(a):
            return 1 if first_unit(a) else 4 * a

        def h_his(a, last=False):
            return 4 * a + 5 - int(last)

        def att_use(a, j):
            return j if first_unit(a) else 4 * a - 2 + j

        def fc2_use(f, j, last=False):
            return 4 * f + 4 + j - 2 * int(last)

        HP = M // 2

        K_AT, WQ_AT = 1, 1 + K
        V_AT = WQ_AT + 2
        M0_AT = V_AT + K
        VEC_AT = M0_AT + 2 * C
        VW_AT = VEC_AT + 1
        M1_AT = VW_AT + B * JC // 2
        B1_AT = M1_AT + 2 * C
        assert B == 2 and B * JC % 2 == 0 and K == 4

        def prep_bank(use):
            return (hid + tok)[use % 4] if use < M1_AT else hid[use % 2]

        def freed_up_to(use):
            return use - sum(WQ_AT <= u < V_AT for u in range(use))

        def prep_done_before(use):
            return max((freed_up_to(u + 1) for u in range(use) if prep_bank(u) is prep_bank(use)), default=0)

        with nc.Block() as block:

            @block.sync
            def _(sp):
                sp.dma_start(ctx_sb[:, :, :], ctx_v).then_inc(ctx_in_sem, 16)
                sp.dma_start(wq_sb[:, :, :], wq.rearrange("(n p) f -> p n f", p=P)).then_inc(wq_in, 16)
                sp.dma_start(wv_sb[:, :, :], wv.rearrange("(n p) f -> p n f", p=CC)).then_inc(wv_in, 16)
                sp.dma_start(wo_sb[:, :, :], wo.rearrange("(n p) f -> p n f", p=P)).then_inc(wo_in, 16)
                sp.dma_start(bo_sb[:, :], bo.rearrange("(o e) -> o e", o=1)).then_inc(bo_in, 16)
                sp.dma_start(x_sb[:, UT:2 * UT, :], x_v[:, UT:2 * UT, :]).then_inc(x1_in, 16)
                sp.dma_start(q1_sb[:, :, :], q1.rearrange("(n p) f -> p n f", p=P)).then_inc(q1_in, 16)
                for c in range(C):
                    sp.dma_start(w1_sb[:, c, :], s1[c:c + 1, :].to_broadcast([P, F])).then_inc(s1_in, 16)
                sp.dma_start(q2_sb[:, :, :], q2.rearrange("(n p) f -> p n f", p=P)).then_inc(q2_in, 16)
                sp.dma_start(w2_sb[:, :, :], s2.rearrange("(o m) e -> o m e", o=1).to_broadcast([P, M, D])).then_inc(s2_in, 16)
                sp.dma_start(x_sb[:, 2 * UT:NT, :], x_v[:, 2 * UT:NT, :]).then_inc(x_rest_in, 16)

                def store(f, last=False):
                    for j in range(UT):
                        sp.wait_ge(tok_freed, fc2_use(f, j, last) + 1)
                        t = f * UT + j
                        sp.dma_start(out_v[:, bass.ds(t, 1), :], x_sb[:, bass.ds(t, 1), :]).then_inc(stored, 16)

                with sp.Fori(0, LAST) as f:
                    store(f)
                store(LAST, last=True)
                sp.wait_ge(stored, 16 * NT)

            @block.gpsimd
            def _(pool):
                nc.gpsimd.memset(ident[:, :], 0.0).then_inc(zeroed, 1)
                pool.wait_ge(zeroed, 1)
                nc.gpsimd.affine_select(out=ident[:, :], in_=ident[:, :], compare_op=ALU.not_equal, fill=1.0,
                                        base=0, pattern=[[-1, P]], channel_multiplier=1).then_inc(const_ready, 1)
                nc.gpsimd.memset(neg_half[:, :], -0.5).then_inc(const_ready, 1)
                nc.gpsimd.memset(kT[:, :, :, :], 0.0).then_inc(zeroed, 1)
                nc.gpsimd.memset(bias_hot[:, :], 0.0).then_inc(zeroed, 1)
                nc.gpsimd.memset(probs[:, :, HJ:JC * P], 0.0).then_inc(zeroed, 1)
                pool.wait_ge(zeroed, 4)
                nc.gpsimd.memset(bias_hot[:, BIAS_ROW:BIAS_ROW + 1], 1.0).then_inc(const_ready, 1)
                nc.gpsimd.memset(probs[:, :, HJ:HJ + 1], 1.0).then_inc(const_ready, 1)
                nc.gpsimd.memset(vT[:, :, :, :], 0.0).then_inc(vT_zeroed, 1)
                pool.wait_ge(const_ready, 4)

                def rsqrt1(n, t0, t1):
                    pool.wait_ge(mv1_done, t1)
                    nc.gpsimd.tensor_scalar(veps1[:, t0:t1], mv1[:, t0:t1, 1], EPS, None, ALU.add).then_inc(veps1_done, 1)
                    pool.wait_ge(veps1_done, n)
                    nc.gpsimd.tensor_tensor(rstd1[:, t0:t1], veps1[:, t0:t1], neg_half[:, t0:t1],
                                            ALU.pow).then_inc(rstd1_done, 1)

                rsqrt1(1, 0, UT)
                pool.wait_ge(b2_in, 16)
                nc.gpsimd.tensor_scalar(b2_half[:, :], b2_sb[:, :], 0.5, None, ALU.mult).then_inc(b2_done, 1)
                pool.wait_ge(w1_shifted, 1)
                pool.wait_ge(s1_in, 16 * C)
                nc.gpsimd.tensor_tensor(w1_sb[:, :, :], f32(q1_sb[:, :, :]), w1_sb[:, :, :], ALU.mult).then_inc(w1_done, 1)
                rsqrt1(2, UT, 2 * UT)

                def normalize(a):
                    for j in range(UT):
                        wait_alone(pool, rsum_done, a * UT + j + 1)
                        p = probs[:, j, 0:HJ].rearrange("p (h j) -> p h j", h=HEADS)
                        nc.gpsimd.tensor_tensor(p, p, rsum[:, j, :].unsqueeze(2).to_broadcast([P, HEADS, J]),
                                                ALU.mult).then_inc(norm_done, 1)

                def rsqrt2(a):
                    wait_alone(pool, mv2_done, a * UT + UT)
                    nc.gpsimd.tensor_scalar(vars2[:, 0, :], mv2[:, :, 1], EPS, None, ALU.add).then_inc(vars2_done, 1)
                    nc.gpsimd.tensor_scalar(vars2[:, 1, :], mv2[:, :, 1], 1.0 + EPS, EPS * EPS,
                                            ALU.mult, ALU.add).then_inc(vars2_done, 1)
                    wait_alone(pool, vars2_done, a * 2 + 2)
                    nc.gpsimd.tensor_tensor(rstd2[:, :, :].rearrange("p a b -> p (a b)"),
                                            vars2[:, :, :].rearrange("p a b -> p (a b)"),
                                            neg_half[:, 0:2 * UT], ALU.pow).then_inc(rstd2_done, 1)

                def residual(f):
                    wait_alone(pool, ln_done, f * UT + UT)
                    r = x_sb[:, bass.ds(f * UT, UT), :]
                    nc.gpsimd.tensor_tensor(r, r, ln[:, :, :], ALU.add).then_inc(res_part, 1)
                    wait_alone(pool, res_part, f + 1)
                    nc.gpsimd.tensor_tensor(r, r, b2_half[:, :].unsqueeze(1).to_broadcast([P, UT, D]),
                                            ALU.add).then_inc(res_done, 1)

                def lower_y(f, pairs=range(HP)):
                    for p in pairs:
                        pool.wait_ge(y_hi_done, f * HP + p + 1)
                        two = slice(2 * p, 2 * p + 2)
                        nc.gpsimd.tensor_tensor(y_lo[:, two, :], y[:, two, :], f32(y_hi[:, two, :]),
                                                ALU.subtract).then_inc(y_lo_done, 1)

                normalize(0)
                pool.wait_ge(w1_hi_done, 1)
                nc.gpsimd.tensor_tensor(w1_lo[:, :, :], w1_sb[:, :, :], f32(w1_hi[:, :, :]),
                                        ALU.subtract).then_inc(w1_split, 1)
                pool.wait_ge(s2_in, 16)
                for n in range(2):
                    half = slice(n * M // 2, (n + 1) * M // 2)
                    pool.wait_ge(w2_shifted, n + 1)
                    nc.gpsimd.tensor_tensor(w2_sb[:, half, :], f32(q2_sb[:, half, :]), w2_sb[:, half, :],
                                            ALU.mult).then_inc(w2_done, 1)
                pool.wait_ge(b2_done, 1)
                rsqrt2(0)
                rsqrt1(3, 2 * UT, 3 * UT)
                pool.wait_ge(w2_hi_done, 1)
                nc.gpsimd.tensor_tensor(w2_lo[:, :, :], w2_sb[:, :, :], f32(w2_hi[:, :, :]),
                                        ALU.subtract).then_inc(w2_split, 1)

                def step(a, last=False):
                    residual(a - 1)
                    normalize(a)
                    lower_y(a - 1, range(HP - int(last)))
                    rsqrt2(a)
                    if last:
                        lower_y(a - 1, range(HP - 1, HP))

                normalize(1)
                residual(0)
                lower_y(0)
                rsqrt2(1)
                rsqrt1(4, 3 * UT, NT)
                with pool.Fori(2, LAST) as a:
                    step(a)
                step(LAST, last=True)
                residual(LAST)

            @block.scalar
            def _(act):
                act.dma_start(wk_sb[:, :, :], wk.rearrange("(n p) f -> p n f", p=CC)).then_inc(wk_in, 16)
                act.dma_start(x_sb[:, 0:UT, :], x_v[:, 0:UT, :]).then_inc(x0_in, 16)
                act.wait_ge(const_ready, 2)
                nc.scalar.activation(table_probe[:, :], neg_half[:, 0:1], ACT.Exp)
                act.dma_start(vec_rows[0:C, :], gamma.rearrange("(n p) -> n p", p=P)).then_inc(vec_in, 16)
                act.dma_start(vec_rows[C:2 * C, :], beta.rearrange("(n p) -> n p", p=P)).then_inc(vec_in, 16)
                act.dma_start(vec_rows[2 * C:2 * C + M, :], b1.rearrange("(n p) -> n p", p=P)).then_inc(vec_in, 16)
                act.dma_start(b2_sb[:, :], b2.rearrange("(o e) -> o e", o=1).to_broadcast([P, D])).then_inc(b2_in, 16)

                def prep_hi(use, dst, src, scale):
                    act.wait_ge(prep_filled, use + 1)
                    nc.scalar.activation(dst, src, ACT.Copy, scale=scale).then_inc(prep_hi_done, 1)

                def m_hi_parts(b, at, parts=range(2 * C)):
                    for n in parts:
                        c, h = n // 2, n % 2
                        prep_hi(at + n, m_hi[:, b, c, h, :], prep_bank(at + n)[:, 0:HALF], DH ** -0.5)

                def vw_hi_part(n):
                    prep_hi(VW_AT + n, vw_hi[:, 2 * n:2 * n + 2, :], prep_bank(VW_AT + n)[:, :], 1.0)

                def exponentials(a, j):
                    act.wait_ge(work_freed, score_use(a, j) + 1)
                    nc.scalar.activation(probs[:, j, 0:HJ], probs[:, j, 0:HJ], ACT.Exp).then_inc(exp_done, 1)

                def work_hi(use, slot, dst, width):
                    act.wait_ge(work_filled, use + 1)
                    nc.scalar.activation(dst, work[slot][:, 0:width], ACT.Copy).then_inc(work_hi_done, 1)

                def h_hi(a, slot=H_SLOT, last=False):
                    act.wait_ge(work_filled, h_use(a, last) + 1)
                    for c in range(C):
                        ins = nc.scalar.activation(hT_hi[:, c, :], work[slot][:, c * W:(c + 1) * W], ACT.Copy,
                                                   scale=gamma_sb[:, c:c + 1])
                    ins.then_inc(work_hi_done, 1)

                def flat(t):
                    return t.rearrange("p a b -> p (a b)")

                def x_hi(a, slot=X_SLOT):
                    work_hi(x_use(a), slot, flat(xT_hi[:, :, :]), C * W)

                def prob_hi(a, j):
                    work_hi(prob_use(a, j), PROB_SLOT[j], flat(pT_hi[:, j, :, :]), JC * P)

                def hidden(f, p, first=False):
                    act.wait_ge(hid_filled, f * HP + p + 1)
                    if not first:
                        act.wait_ge(y_lo_done, f * HP + p + 1 - HP)
                    for q in range(2):
                        m = 2 * p + q
                        last = nc.scalar.activation(y[:, m, :], hid[p % 2][:, q * W:(q + 1) * W], ACT.Silu,
                                                    bias=b1_eff[:, m:m + 1])
                    last.then_inc(silu_done, 1)
                    act.wait_ge(silu_done, f * HP + p + 1)
                    nc.scalar.activation(y_hi[:, 2 * p:2 * p + 2, :], y[:, 2 * p:2 * p + 2, :],
                                         ACT.Copy).then_inc(y_hi_done, 1)

                for n in range(2):
                    act.wait_ge(prep_filled, WQ_AT + n + 1)
                    nc.scalar.activation(wqT[:, 2 * n:2 * n + 2, :],
                                         prep_bank(WQ_AT + n)[:, :].rearrange("p (k e) -> p k e", k=2),
                                         ACT.Copy).then_inc(wqT_done, 1)
                m_hi_parts(0, M0_AT)
                x_hi(0, slot=0)
                act.wait_ge(q1_in, 16)
                nc.scalar.activation(f32(q1_sb[:, :, :]), q1_sb[:, :, :], ACT.Copy, bias=-ZERO_POINT).then_inc(w1_shifted, 1)
                vw_hi_part(0)
                act.wait_ge(prep_freed, freed_up_to(VEC_AT + 1))
                nc.scalar.activation(beta_parts[:, :, 0], beta_sb, ACT.Copy).then_inc(beta_hi_done, 1)
                exponentials(0, 0)
                exponentials(0, 1)
                vw_hi_part(1)
                vw_hi_part(2)
                act.wait_ge(w1_done, 1)
                nc.scalar.activation(w1_hi[:, :, :], w1_sb[:, :, :], ACT.Copy).then_inc(w1_hi_done, 1)
                for n in range(3, B * JC // 2):
                    vw_hi_part(n)
                prob_hi(0, 0)
                prob_hi(0, 1)
                m_hi_parts(1, M1_AT, range(2))
                x_hi(1)
                act.wait_ge(q2_in, 16)
                for half in (slice(0, M // 2), slice(M // 2, M)):
                    nc.scalar.activation(f32(q2_sb[:, half, :]), q2_sb[:, half, :], ACT.Copy,
                                         bias=-ZERO_POINT).then_inc(w2_shifted, 1)
                m_hi_parts(1, M1_AT, range(2, 2 * C))
                act.wait_ge(w2_done, 2)
                nc.scalar.activation(w2_hi[:, :, :], w2_sb[:, :, :], ACT.Copy).then_inc(w2_hi_done, 1)

                def step(a, first=False, last=False):
                    exponentials(a, 0)
                    h_hi(a - 1)
                    exponentials(a, 1)
                    nc.scalar.activation(table_probe[:, :], neg_half[:, 0:1], ACT.Silu)
                    if first:
                        act.wait_ge(prep_freed, freed_up_to(B1_AT + 1))
                    hidden(a - 1, 0, first)
                    hidden(a - 1, 1, first)
                    prob_hi(a, 0)
                    prob_hi(a, 1)
                    hidden(a - 1, 2, first)
                    hidden(a - 1, 3, first)
                    if not last:
                        x_hi(a + 1)

                step(1, first=True)
                with act.Fori(2, LAST) as a:
                    step(a)
                step(LAST, last=True)
                h_hi(LAST, slot=1, last=True)
                for p in range(HP):
                    hidden(LAST, p)

            @block.vector
            def _(dve):
                def stats1(t):
                    nc.vector.bn_stats(bn1[:, t, :], x_sb[:, t, :]).then_inc(bn1_done, 1)
                    dve.wait_ge(bn1_done, t + 1)
                    nc.vector.bn_aggr(mv1[:, t, :], bn1[:, t, :]).then_inc(mv1_done, 1)

                def normalize_x(a):
                    for j in range(UT):
                        t = a * UT + j
                        ins = nc.vector.tensor_scalar(xn[:, j, :], x_sb[:, bass.ds(t, 1), :], mv1[:, bass.ds(t, 1), 0],
                                                      rstd1[:, bass.ds(t, 1)], ALU.subtract, ALU.mult)
                    ins.then_inc(xn_done, 1)

                def prep_wait(use):
                    dve.wait_ge(prep_filled, use + 1)
                    return prep_bank(use)

                def m_lo_parts(b, at, parts=range(2 * C)):
                    for n in parts:
                        c, h = n // 2, n % 2
                        dve.wait_ge(prep_hi_done, b * (2 * C + B * JC // 2) + n + 1)
                        nc.vector.scalar_tensor_tensor(m_lo[:, b, c, h, :], prep_bank(at + n)[:, 0:HALF], DH ** -0.5,
                                                       f32(m_hi[:, b, c, h, :]), ALU.mult,
                                                       ALU.subtract).then_inc(prep_freed, 1)

                def vw_lo_part(n):
                    dve.wait_ge(prep_hi_done, 2 * C + n + 1)
                    nc.vector.tensor_tensor(vw_lo[:, 2 * n:2 * n + 2, :],
                                            prep_bank(VW_AT + n)[:, :].rearrange("p (m e) -> p m e", m=2),
                                            f32(vw_hi[:, 2 * n:2 * n + 2, :]), ALU.subtract).then_inc(prep_freed, 1)

                def flat(t):
                    return t.rearrange("p a b -> p (a b)")

                def work_lo(his, slot, dst, hi, width):
                    dve.wait_ge(work_hi_done, his)
                    nc.vector.tensor_tensor(dst, work[slot][:, 0:width], f32(hi), ALU.subtract).then_inc(work_freed, 1)

                def shift_scores(a, j):
                    dve.wait_ge(work_filled, score_use(a, j) + 1)
                    s = work[score_slot(a, j)][:, :].rearrange("p (n c) -> p n c", n=2)[:, :, 0:HALF]
                    s = s.rearrange("p n (h j) -> p n h j", j=J)
                    mx = smax[:, j, :].rearrange("p (n h) -> p n h", n=2)
                    nc.vector.tensor_reduce(mx, s, AX_X, ALU.max).then_inc(max_done, 1)
                    dve.wait_ge(max_done, a * UT + j + 1)
                    nc.vector.tensor_tensor(probs[:, j, 0:HJ].rearrange("p (n h j) -> p n h j", n=2, j=J), s,
                                            mx.unsqueeze(3).to_broadcast([P, 2, HEADS // 2, J]),
                                            ALU.subtract).then_inc(work_freed, 1)

                def invert_sums(a, j):
                    dve.wait_ge(exp_done, a * UT + j + 1)
                    nc.vector.tensor_reduce(ssum[:, j, :], probs[:, j, 0:HJ].rearrange("p (h j) -> p h j", h=HEADS),
                                            AX_X, ALU.add).then_inc(sum_done, 1)
                    dve.wait_ge(sum_done, a * UT + j + 1)
                    nc.vector.reciprocal(rsum[:, j, :], ssum[:, j, :]).then_inc(rsum_done, 1)

                def x_lo(a, slot=X_SLOT):
                    work_lo(x_his(a), slot, flat(xT_lo[:, :, :]), flat(xT_hi[:, :, :]), C * W)

                def h_lo(a, slot=H_SLOT, last=False):
                    dve.wait_ge(work_hi_done, h_his(a, last))
                    for c in range(C):
                        ins = nc.vector.scalar_tensor_tensor(hT_lo[:, c, :], work[slot][:, c * W:(c + 1) * W],
                                                             gamma_sb[:, c:c + 1], f32(hT_hi[:, c, :]), ALU.mult, ALU.subtract)
                    ins.then_inc(work_freed, 1)

                def prob_lo(a, j):
                    work_lo(prob_his(a, j), PROB_SLOT[j], flat(pT_lo[:, j, :, :]), flat(pT_hi[:, j, :, :]), JC * P)

                def add_attention(a, j):
                    use = att_use(a, j)
                    x2 = x_sb[:, bass.ds(a * UT + j, 1), :]
                    dve.wait_ge(tok_filled, use + 1)
                    nc.vector.tensor_tensor(x2, tok[j][:, 0:D].unsqueeze(1), x2, ALU.add).then_inc(tok_freed, 1)
                    wait_alone(dve, tok_freed, use + 1)
                    nc.vector.bn_stats(bn2[:, j, :], x2).then_inc(bn2_done, 1)
                    wait_alone(dve, bn2_done, a * UT + j + 1)
                    nc.vector.bn_aggr(mv2[:, j, :], bn2[:, j, :]).then_inc(mv2_done, 1)

                def normalized_x2(a, j, dst, n):
                    return nc.vector.tensor_scalar(dst[:, j, :].unsqueeze(1), x_sb[:, bass.ds(a * UT + j, 1), :],
                                                   mv2[:, j, 0:1], rstd2[:, n, j:j + 1], ALU.subtract, ALU.mult)

                def make_hn(a):
                    dve.wait_ge(rstd2_done, a + 1)
                    for j in range(UT):
                        normalized_x2(a, j, hn, 1).then_inc(hn_done, 1)

                def make_ln(a, first=False):
                    if not first:
                        dve.wait_ge(res_done, a)
                    for j in range(UT):
                        normalized_x2(a, j, ln, 0).then_inc(ln_done, 1)

                def finish_tile(f, j, last=False):
                    dve.wait_ge(tok_filled, fc2_use(f, j, last) + 1)
                    dve.wait_ge(res_done, f + 1)
                    o = x_sb[:, bass.ds(f * UT + j, 1), :]
                    nc.vector.scalar_tensor_tensor(o, tok[j][:, 0:D].unsqueeze(1), 0.5, o, ALU.mult,
                                                   ALU.add).then_inc(tok_freed, 1)

                nc.vector.tensor_copy(ctxT[:, :, :], prep_wait(0)[0:CC, 0:2 * BJ].rearrange("p (n j) -> p n j", n=2)
                                      ).then_inc(prep_freed, 1)
                dve.wait_ge(zeroed, 4)
                for k in range(K):
                    r = prep_wait(K_AT + k)[:, 0:BJ].rearrange("p (b j) -> p b j", b=B)
                    nc.vector.tensor_copy(kT[0:DH, k, :, 0:J], r[0:DH, :, :])
                    nc.vector.tensor_copy(kT[DH:P, k, :, J:PAIR], r[DH:P, :, :]).then_inc(prep_freed, 1)
                dve.wait_ge(x0_in, 16)
                for t in range(UT):
                    stats1(t)
                dve.wait_ge(vT_zeroed, 1)
                for k in range(K):
                    r = prep_wait(V_AT + k)[:, 0:BJ].rearrange("p (b j) -> p b j", b=B)
                    at = k * PAIR - chunk0[k] * P
                    nc.vector.tensor_copy(vT[0:DH, k, :, at:at + J], r[0:DH, :, :])
                    nc.vector.tensor_copy(vT[DH:P, k, :, at + J:at + PAIR], r[DH:P, :, :]).then_inc(prep_freed, 1)
                dve.wait_ge(mv1_done, UT)
                dve.wait_ge(rstd1_done, 1)
                normalize_x(0)
                m_lo_parts(0, M0_AT)
                x_lo(0, slot=0)
                nc.vector.tensor_copy(vec_cols[:, :], prep_wait(VEC_AT)[:, 0:2 * C + M]).then_inc(prep_freed, 1)
                vw_lo_part(0)
                dve.wait_ge(x1_in, 16)
                for t in range(UT, 2 * UT):
                    stats1(t)
                shift_scores(0, 0)
                shift_scores(0, 1)
                dve.wait_ge(beta_hi_done, 1)
                nc.vector.tensor_tensor(beta_parts[:, :, 1], beta_sb, f32(beta_parts[:, :, 0]),
                                        ALU.subtract).then_inc(beta_split, 1)
                invert_sums(0, 0)
                invert_sums(0, 1)
                for n in range(1, B * JC // 2):
                    vw_lo_part(n)
                    if n == 1:
                        dve.wait_ge(work_filled, x_use(0) + 1)
                        dve.wait_ge(mv1_done, 2 * UT)
                        dve.wait_ge(rstd1_done, 2)
                        normalize_x(1)
                prob_lo(0, 0)
                prob_lo(0, 1)
                m_lo_parts(1, M1_AT, range(2))
                x_lo(1)
                dve.wait_ge(x_rest_in, 16)
                for t in range(2 * UT, 3 * UT):
                    stats1(t)
                add_attention(0, 0)
                add_attention(0, 1)
                m_lo_parts(1, M1_AT, range(2, 2 * C))
                shift_scores(1, 0)
                make_hn(0)
                shift_scores(1, 1)

                def step(a, first=False, last=False):
                    if not first:
                        shift_scores(a, 0)
                        shift_scores(a, 1)
                    h_lo(a - 1)
                    if first:
                        make_ln(0, first=True)
                        r = prep_wait(B1_AT)[:, 0:2 * M].rearrange("p (m n) -> p m n", n=2)
                        nc.vector.tensor_tensor(b1_part[:, :], r[:, :, 0], b1_sb, ALU.add).then_inc(b1_part_done, 1)
                        dve.wait_ge(b1_part_done, 1)
                        nc.vector.tensor_tensor(b1_eff[:, :], r[:, :, 1], b1_part[:, :], ALU.add).then_inc(prep_freed, 1)
                    invert_sums(a, 0)
                    invert_sums(a, 1)
                    if not first:
                        finish_tile(a - 2, 1)
                    if first:
                        dve.wait_ge(mv1_done, 3 * UT)
                        dve.wait_ge(rstd1_done, 3)
                    if not last:
                        normalize_x(a + 1)
                    if first:
                        for t in range(3 * UT, NT - 2 * UT):
                            stats1(t)
                    prob_lo(a, 0)
                    prob_lo(a, 1)
                    if first:
                        for t in range(NT - 2 * UT, NT):
                            stats1(t)
                    add_attention(a, 0)
                    add_attention(a, 1)
                    if not last:
                        x_lo(a + 1)
                    make_hn(a)
                    make_ln(a)
                    finish_tile(a - 1, 0)

                step(1, first=True)
                dve.wait_ge(mv1_done, NT)
                dve.wait_ge(rstd1_done, 4)
                with dve.Fori(2, LAST) as a:
                    step(a)
                step(LAST, last=True)
                h_lo(LAST, slot=1, last=True)
                finish_tile(LAST - 1, 1)
                for p in range(HP):
                    dve.wait_ge(y_lo_done, LAST * HP + p)
                    dve.wait_ge(y_hi_done, LAST * HP + p + 1)
                    two = slice(2 * p, 2 * p + 2)
                    nc.vector.tensor_tensor(y_lo[:, two, :], y[:, two, :], f32(y_hi[:, two, :]),
                                            ALU.subtract).then_inc(y_lo_done, 1)
                finish_tile(LAST, 0, last=True)
                finish_tile(LAST, 1, last=True)

            @block.tensor
            def _(pe):
                mm = nc.tensor.matmul

                def transposes(slot, src, use):
                    if not (isinstance(use, int) and use < 2):
                        pe.wait_ge(work_freed, use - 1)
                    for j in range(UT):
                        for c in range(C):
                            ins = nc.tensor.transpose(work[slot][:, c * W + j * P:c * W + (j + 1) * P],
                                                      src[:, j, c * P:(c + 1) * P], ident[:, :])
                    ins.then_inc(work_filled, 1)

                def scores(a, j, b):
                    if not (isinstance(a, int) and score_use(a, j) < 2):
                        pe.wait_ge(work_freed, score_use(a, j) - 1)
                    if j == 0:
                        pe.wait_ge(work_freed, x_use(a) + 1)
                    for h in range(2):
                        o = work[score_slot(a, j)][:, h * BANK:h * BANK + HALF]
                        steps = [(xt, m, c) for c in range(C) for xt, m in ((xT_hi, m_hi), (xT_hi, m_lo), (xT_lo, m_hi))]
                        for n, (xt, m, c) in enumerate(steps):
                            ins = mm(o, xt[:, c, j * P:(j + 1) * P], m[:, b, c, h, :], start=n == 0, stop=n == len(steps) - 1)
                    ins.then_inc(work_filled, 1)

                def prob_transposes(a, j):
                    pe.wait_ge(norm_done, a * UT + j + 1)
                    pe.wait_ge(work_freed, prob_use(a, j) - 1)
                    for m in range(JC):
                        ins = nc.tensor.transpose(work[PROB_SLOT[j]][:, m * P:(m + 1) * P], probs[:, j, m * P:(m + 1) * P],
                                                  ident[:, :])
                    ins.then_inc(work_filled, 1)

                def attention_out(a, j, b, first=False):
                    if not first:
                        pe.wait_ge(tok_freed, att_use(a, j) - 1)
                    pe.wait_ge(work_freed, prob_use(a, j) + 1)
                    steps = [(p, v, m) for m in range(JC) for p, v in ((pT_hi, vw_hi), (pT_hi, vw_lo), (pT_lo, vw_hi))]
                    for n, (p, v, m) in enumerate(steps):
                        ins = mm(tok[j][:, 0:D], p[:, j, m, :], v[:, b * JC + m, :], start=n == 0, stop=n == len(steps) - 1)
                    ins.then_inc(tok_filled, 1)

                def fc1_pair(f, p, first=False, last=False):
                    if p == 0:
                        pe.wait_ge(work_freed, h_use(f, last) + 1)
                    if not (first and p < 2):
                        pe.wait_ge(silu_done, f * HP + p - 1)
                    steps = [(w, h, c) for c in range(C) for w, h in ((w1_hi, hT_hi), (w1_hi, hT_lo), (w1_lo, hT_hi))]
                    for q in range(2):
                        m = 2 * p + q
                        for n, (w, h, c) in enumerate(steps):
                            ins = mm(hid[p % 2][:, q * W:(q + 1) * W], w[:, c, m * P:(m + 1) * P], h[:, c, :],
                                     start=n == 0, stop=n == len(steps) - 1)
                    ins.then_inc(hid_filled, 1)

                def fc2(f, j, chunks=range(M), last=False):
                    if chunks[0] == 0:
                        pe.wait_ge(tok_freed, fc2_use(f, j, last) - 1)
                    for m in chunks:
                        if m % 2 == 0 or m == chunks[0]:
                            pe.wait_ge(y_lo_done, f * HP + m // 2 + 1)
                        for n, (s, w) in enumerate(((y_hi, w2_hi), (y_hi, w2_lo), (y_lo, w2_hi))):
                            ins = mm(tok[j][:, 0:D], s[:, m, j * P:(j + 1) * P], w[:, m, :],
                                     start=m == 0 and n == 0, stop=m == M - 1 and n == 2)
                    if chunks[-1] == M - 1:
                        ins.then_inc(tok_filled, 1)

                def emptied(use):
                    if prep_done_before(use):
                        pe.wait_ge(prep_freed, prep_done_before(use))
                    if V_AT <= use < V_AT + K and WQ_AT <= use - 4 < V_AT:
                        pe.wait_ge(wqT_done, use - 4 - WQ_AT + 1)
                    return prep_bank(use)

                def project(at, w):
                    for k in range(K):
                        r = emptied(at + k)
                        for n in range(2):
                            ins = mm(r[:, 0:BJ], w[:, n, k * P:(k + 1) * P], ctxT[:, n, :], start=n == 0, stop=n == 1)
                        ins.then_inc(prep_filled, 1)

                def make_m(b, at, parts=range(2 * C)):
                    for n in parts:
                        c, h = n // 2, n % 2
                        r = emptied(at + n)
                        for q in range(2):
                            k = 2 * h + q
                            ins = mm(r[:, q * PAIR:(q + 1) * PAIR], wqT[:, k, c * P:(c + 1) * P], kT[:, k, b, :],
                                     start=True, stop=True)
                        ins.then_inc(prep_filled, 1)

                def warm(n):
                    for _ in range(n):
                        nc.tensor.transpose(work[1][:, 0:P], ident[:, :], ident[:, :])

                def make_vw(banks):
                    for n in banks:
                        r = emptied(VW_AT + n)
                        for q in range(2):
                            b, m = divmod(2 * n + q, JC)
                            o = r[:, q * D:(q + 1) * D]
                            ks = [k for k in range(K) if k * PAIR < (m + 1) * P and (k + 1) * PAIR > m * P]
                            assert all(0 <= m - chunk0[k] < 2 for k in ks)
                            for k in ks:
                                n0 = (m - chunk0[k]) * P
                                ins = mm(o, vT[:, k, b, n0:n0 + P], wo_sb[:, k, :], start=k == ks[0],
                                         stop=k == ks[-1] and m < JC - 1)
                            if m == JC - 1:
                                ins = mm(o, bias_hot[0:1, :], bo_sb[0:1, :], start=False, stop=True)
                        ins.then_inc(prep_filled, 1)

                pe.wait_ge(const_ready, 1)
                warm(WARM[0])
                pe.wait_ge(ctx_in_sem, 16)
                r = emptied(0)
                for n in range(2):
                    for b in range(B):
                        at = n * BJ + b * J
                        ins = nc.tensor.transpose(r[0:CC, at:at + J], ctx_sb[:, b, n * CC:(n + 1) * CC], ident[0:J, 0:J])
                ins.then_inc(prep_filled, 1)
                warm(WARM[1])
                pe.wait_ge(wk_in, 16)
                pe.wait_ge(prep_freed, 1)
                project(K_AT, wk_sb)
                pe.wait_ge(wq_in, 16)
                for n in range(2):
                    r = emptied(WQ_AT + n)
                    for q in range(2):
                        for c in range(C):
                            k = 2 * n + q
                            ins = nc.tensor.transpose(r[:, q * D + c * P:q * D + (c + 1) * P],
                                                      wq_sb[:, c, k * P:(k + 1) * P], ident[:, :])
                    ins.then_inc(prep_filled, 1)
                pe.wait_ge(wv_in, 16)
                project(V_AT, wv_sb)
                pe.wait_ge(prep_freed, freed_up_to(WQ_AT))
                pe.wait_ge(wqT_done, 2)
                make_m(0, M0_AT)
                pe.wait_ge(xn_done, 1)
                transposes(0, xn, x_use(0))
                pe.wait_ge(vec_in, 16 * 3)
                NV = 2 * C + M
                nc.tensor.transpose(emptied(VEC_AT)[:, 0:NV], vec_rows[:, :], ident[0:NV, 0:NV]).then_inc(prep_filled, 1)
                pe.wait_ge(wo_in, 16)
                pe.wait_ge(const_ready, 4)
                pe.wait_ge(bo_in, 16)
                pe.wait_ge(prep_freed, freed_up_to(M0_AT))
                make_vw(range(1))
                pe.wait_ge(prep_freed, freed_up_to(VEC_AT))
                scores(0, 0, 0)
                scores(0, 1, 0)
                make_vw(range(1, B * JC // 2))
                prob_transposes(0, 0)
                prob_transposes(0, 1)
                make_m(1, M1_AT, range(2))
                pe.wait_ge(xn_done, 2)
                transposes(X_SLOT, xn, x_use(1))
                pe.wait_ge(prep_freed, freed_up_to(M1_AT))
                attention_out(0, 0, 0, first=True)
                attention_out(0, 1, 0, first=True)
                make_m(1, M1_AT, range(2, 2 * C))

                def step(a, b, first=False, last=False):
                    scores(a, 0, b)
                    scores(a, 1, b)

                    def h_transposes():
                        pe.wait_ge(hn_done, a * UT)
                        transposes(H_SLOT, hn, h_use(a - 1))

                    if first:
                        pe.wait_ge(beta_split, 1)
                        pe.wait_ge(w1_split, 1)
                        r = emptied(B1_AT)
                        for m in range(M):
                            if m == 3:
                                h_transposes()
                            steps = [(w, c) for w in (w1_hi, w1_lo) for c in range(C)]
                            for n, (w, c) in enumerate(steps):
                                ins = mm(r[:, 2 * m:2 * m + 2], w[:, c, m * P:(m + 1) * P], beta_parts[:, c, :],
                                         start=n == 0, stop=n == len(steps) - 1)
                        ins.then_inc(prep_filled, 1)
                        assert prep_bank(B1_AT) is hid[1]
                        pe.wait_ge(prep_freed, freed_up_to(B1_AT))
                    else:
                        fc2(a - 2, 1, range(2))
                        h_transposes()
                        fc2(a - 2, 1, range(2, M))
                    fc1_pair(a - 1, 0, first)
                    if first:
                        pe.wait_ge(prep_freed, freed_up_to(B1_AT + 1))
                    fc1_pair(a - 1, 1, first)
                    prob_transposes(a, 0)
                    prob_transposes(a, 1)
                    fc1_pair(a - 1, 2)
                    fc1_pair(a - 1, 3)
                    attention_out(a, 0, b)
                    attention_out(a, 1, b)
                    if not last:
                        pe.wait_ge(xn_done, a + 2)
                        transposes(X_SLOT, xn, x_use(a + 1))
                    if first:
                        pe.wait_ge(w2_split, 1)
                    if not last:
                        fc2(a - 1, 0)

                step(1, 0, first=True)
                with pe.Fori(2, UB) as a:
                    step(a, 0)
                with pe.Fori(UB, LAST) as a:
                    step(a, 1)
                step(LAST, 1, last=True)

                fc2(LAST - 1, 0, range(M - 2))
                fc2(LAST - 1, 1, range(EARLY))
                pe.wait_ge(hn_done, NT)
                transposes(1 - H_SLOT, hn, h_use(LAST, last=True))
                fc2(LAST - 1, 0, range(M - 2, M))
                fc2(LAST - 1, 1, range(EARLY, M))
                for p in range(HP):
                    fc1_pair(LAST, p, last=True)
                for chunks in (range(M - 2), range(M - 2, M)):
                    for j in range(UT):
                        fc2(LAST, j, chunks, last=True)


_INS = ["x", "ctx_768", "L0_xattn_Wq", "L0_xattn_Wk", "L0_xattn_Wv", "L0_xattn_Wo", "L0_xattn_bo",
        "L0_ffn_ln_gamma", "L0_ffn_ln_beta", "L0_ffn_fc1_q", "L0_ffn_fc1_scales", "L0_ffn_fc1_bias",
        "L0_ffn_fc2_q", "L0_ffn_fc2_scales", "L0_ffn_fc2_bias"]


def kernel(**inputs):
    import numpy as _np
    import concourse.bacc as _bacc
    from concourse import mybir as _mybir
    from concourse.bass_utils import run_bass_kernel_spmd as _run

    nc = _bacc.Bacc("TRN2", target_bir_lowering=False, num_devices=1)
    arrays, args = {}, []
    for name in _INS:
        a = _np.ascontiguousarray(inputs[name])
        arrays[f"in_{name}"] = a
        args.append(nc.dram_tensor(f"in_{name}", a.shape, _mybir.dt.from_np(a.dtype), kind="ExternalInput").ap())
    shape = tuple(inputs["x"].shape)
    args.append(nc.dram_tensor("out_x", shape, _mybir.dt.float32, kind="ExternalOutput").ap())
    build_program(nc, *args)
    r = _run(nc, [arrays], core_ids=[0])
    return r.results[0]["out_x"]
```
